# Optimizing a Trainium2 kernel written in Bass

```python
import numpy as np
import jax
import jax.numpy as jnp

def _softmax(x, axis=-1):
    return jax.nn.softmax(x, axis=axis)

def _gelu(x):
    return jax.nn.gelu(x, approximate=True)

def _silu(x):
    return jax.nn.silu(x)

def _sigmoid(x):
    return jax.nn.sigmoid(x)

def _layernorm(x, axis=-1, eps=1e-05):
    m = jnp.mean(x, axis=axis, keepdims=True)
    v = jnp.var(x, axis=axis, keepdims=True)
    return (x - m) / jnp.sqrt(v + eps)

def _scatter_add(tgt, idx, src, axis=0):
    return tgt.at[idx].add(src)

def _segment_sum(src, seg, n):
    return jax.ops.segment_sum(src, seg, n)
kernel_name = 'mk_dlrm_tower_d1_rec_r8_99ea77'

def setup_inputs(seed: int=0):
    np.random.seed(seed)
    _w = jnp.asarray

    def _rec_inputs():
        import jax
        import jax.numpy as jnp
        _tk = jax.random.key(seed)
        ids = jnp.stack([jax.random.randint(jax.random.fold_in(_tk, 200 + f), (512,), 0, v, jnp.int32) for f, v in enumerate([1250, 12500, 1000, 1000, 1000, 1250, 12500, 125000, 12500, 1000, 1000, 1250, 12500, 12500, 1250, 1250, 1250, 1000, 1000, 1250, 1000, 12500, 1000, 1250, 1250, 1250])], axis=1)
        tbl_0 = 0.05 * jax.random.normal(jax.random.fold_in(_tk, 500 + 0), (1250, 128), jnp.float32)
        tbl_1 = 0.05 * jax.random.normal(jax.random.fold_in(_tk, 500 + 1), (12500, 128), jnp.float32)
        tbl_2 = 0.05 * jax.random.normal(jax.random.fold_in(_tk, 500 + 2), (1000, 128), jnp.float32)
        tbl_3 = 0.05 * jax.random.normal(jax.random.fold_in(_tk, 500 + 3), (1000, 128), jnp.float32)
        tbl_4 = 0.05 * jax.random.normal(jax.random.fold_in(_tk, 500 + 4), (1000, 128), jnp.float32)
        tbl_5 = 0.05 * jax.random.normal(jax.random.fold_in(_tk, 500 + 5), (1250, 128), jnp.float32)
        tbl_6 = 0.05 * jax.random.normal(jax.random.fold_in(_tk, 500 + 6), (12500, 128), jnp.float32)
        tbl_7 = 0.05 * jax.random.normal(jax.random.fold_in(_tk, 500 + 7), (125000, 128), jnp.float32)
        tbl_8 = 0.05 * jax.random.normal(jax.random.fold_in(_tk, 500 + 8), (12500, 128), jnp.float32)
        tbl_9 = 0.05 * jax.random.normal(jax.random.fold_in(_tk, 500 + 9), (1000, 128), jnp.float32)
        tbl_10 = 0.05 * jax.random.normal(jax.random.fold_in(_tk, 500 + 10), (1000, 128), jnp.float32)
        tbl_11 = 0.05 * jax.random.normal(jax.random.fold_in(_tk, 500 + 11), (1250, 128), jnp.float32)
        tbl_12 = 0.05 * jax.random.normal(jax.random.fold_in(_tk, 500 + 12), (12500, 128), jnp.float32)
        tbl_13 = 0.05 * jax.random.normal(jax.random.fold_in(_tk, 500 + 13), (12500, 128), jnp.float32)
        tbl_14 = 0.05 * jax.random.normal(jax.random.fold_in(_tk, 500 + 14), (1250, 128), jnp.float32)
        tbl_15 = 0.05 * jax.random.normal(jax.random.fold_in(_tk, 500 + 15), (1250, 128), jnp.float32)
        tbl_16 = 0.05 * jax.random.normal(jax.random.fold_in(_tk, 500 + 16), (1250, 128), jnp.float32)
        tbl_17 = 0.05 * jax.random.normal(jax.random.fold_in(_tk, 500 + 17), (1000, 128), jnp.float32)
        tbl_18 = 0.05 * jax.random.normal(jax.random.fold_in(_tk, 500 + 18), (1000, 128), jnp.float32)
        tbl_19 = 0.05 * jax.random.normal(jax.random.fold_in(_tk, 500 + 19), (1250, 128), jnp.float32)
        tbl_20 = 0.05 * jax.random.normal(jax.random.fold_in(_tk, 500 + 20), (1000, 128), jnp.float32)
        tbl_21 = 0.05 * jax.random.normal(jax.random.fold_in(_tk, 500 + 21), (12500, 128), jnp.float32)
        tbl_22 = 0.05 * jax.random.normal(jax.random.fold_in(_tk, 500 + 22), (1000, 128), jnp.float32)
        tbl_23 = 0.05 * jax.random.normal(jax.random.fold_in(_tk, 500 + 23), (1250, 128), jnp.float32)
        tbl_24 = 0.05 * jax.random.normal(jax.random.fold_in(_tk, 500 + 24), (1250, 128), jnp.float32)
        tbl_25 = 0.05 * jax.random.normal(jax.random.fold_in(_tk, 500 + 25), (1250, 128), jnp.float32)
        _rk = jax.random.fold_in(_tk, 7)
        r_dense_features = -0.000520686 + 1.00062 * jax.random.normal(jax.random.fold_in(_rk, 101), (512, 128), jnp.float32)
        W_top1 = 0.0405887 * jax.random.normal(jax.random.fold_in(_tk, 801), (607, 512), jnp.float32)
        W_top2 = 0.0441942 * jax.random.normal(jax.random.fold_in(_tk, 802), (512, 256), jnp.float32)
        W_top3 = 0.0625 * jax.random.normal(jax.random.fold_in(_tk, 803), (256, 1), jnp.float32)
        b_top1 = jnp.zeros((512,), jnp.float32)
        b_top2 = jnp.zeros((256,), jnp.float32)
        return (r_dense_features, ids, tbl_0, tbl_1, tbl_2, tbl_3, tbl_4, tbl_5, tbl_6, tbl_7, tbl_8, tbl_9, tbl_10, tbl_11, tbl_12, tbl_13, tbl_14, tbl_15, tbl_16, tbl_17, tbl_18, tbl_19, tbl_20, tbl_21, tbl_22, tbl_23, tbl_24, tbl_25, W_top1, b_top1, W_top2, b_top2, W_top3)
    r_dense_features, ids, tbl_0, tbl_1, tbl_2, tbl_3, tbl_4, tbl_5, tbl_6, tbl_7, tbl_8, tbl_9, tbl_10, tbl_11, tbl_12, tbl_13, tbl_14, tbl_15, tbl_16, tbl_17, tbl_18, tbl_19, tbl_20, tbl_21, tbl_22, tbl_23, tbl_24, tbl_25, W_top1, b_top1, W_top2, b_top2, W_top3 = _rec_inputs()

    def _L0_rec_setup():
        import jax, jax.numpy as jnp
        import numpy as np
        NUM_SPARSE = 26
        EMBED_DIM = 128
        BATCH = 2048
        key = jax.random.key(seed)
        k1, k2 = jax.random.split(key)
        dense_features = jax.random.normal(k1, (BATCH, EMBED_DIM), dtype=jnp.float32)
        sparse_features = jax.random.normal(k2, (BATCH, NUM_SPARSE, EMBED_DIM), dtype=jnp.float32)
        return {'dense_features': dense_features, 'sparse_features': sparse_features}
    _L0_rec_all = _L0_rec_setup()
    _L0_rec_in = {k: v for k, v in _L0_rec_all.items() if k in ()}
    del _L0_rec_all
    return {'r_dense_features': r_dense_features, 'ids': ids, 'tbl_0': tbl_0, 'tbl_1': tbl_1, 'tbl_2': tbl_2, 'tbl_3': tbl_3, 'tbl_4': tbl_4, 'tbl_5': tbl_5, 'tbl_6': tbl_6, 'tbl_7': tbl_7, 'tbl_8': tbl_8, 'tbl_9': tbl_9, 'tbl_10': tbl_10, 'tbl_11': tbl_11, 'tbl_12': tbl_12, 'tbl_13': tbl_13, 'tbl_14': tbl_14, 'tbl_15': tbl_15, 'tbl_16': tbl_16, 'tbl_17': tbl_17, 'tbl_18': tbl_18, 'tbl_19': tbl_19, 'tbl_20': tbl_20, 'tbl_21': tbl_21, 'tbl_22': tbl_22, 'tbl_23': tbl_23, 'tbl_24': tbl_24, 'tbl_25': tbl_25, 'W_top1': W_top1, 'b_top1': b_top1, 'W_top2': W_top2, 'b_top2': b_top2, 'W_top3': W_top3}

def reference(r_dense_features, ids, tbl_0, tbl_1, tbl_2, tbl_3, tbl_4, tbl_5, tbl_6, tbl_7, tbl_8, tbl_9, tbl_10, tbl_11, tbl_12, tbl_13, tbl_14, tbl_15, tbl_16, tbl_17, tbl_18, tbl_19, tbl_20, tbl_21, tbl_22, tbl_23, tbl_24, tbl_25, W_top1, b_top1, W_top2, b_top2, W_top3):
    import jax
    import jax.numpy as jnp

    def _L0_rec_ref(dense_features, sparse_features):
        import jax, jax.numpy as jnp
        import numpy as np
        NUM_SPARSE = 26
        EMBED_DIM = 128
        BATCH = 2048
        F = NUM_SPARSE + 1
        combined = jnp.concatenate([dense_features[:, None, :], sparse_features], axis=1)
        interactions = jnp.einsum('bfd,bgd->bfg', combined, combined)
        iu, ju = jnp.triu_indices(F, k=1)
        interactions_flat = interactions[:, iu, ju]
        return jnp.concatenate([dense_features, interactions_flat], axis=1)
    e = jnp.stack([tbl_0[ids[:, 0]], tbl_1[ids[:, 1]], tbl_2[ids[:, 2]], tbl_3[ids[:, 3]], tbl_4[ids[:, 4]], tbl_5[ids[:, 5]], tbl_6[ids[:, 6]], tbl_7[ids[:, 7]], tbl_8[ids[:, 8]], tbl_9[ids[:, 9]], tbl_10[ids[:, 10]], tbl_11[ids[:, 11]], tbl_12[ids[:, 12]], tbl_13[ids[:, 13]], tbl_14[ids[:, 14]], tbl_15[ids[:, 15]], tbl_16[ids[:, 16]], tbl_17[ids[:, 17]], tbl_18[ids[:, 18]], tbl_19[ids[:, 19]], tbl_20[ids[:, 20]], tbl_21[ids[:, 21]], tbl_22[ids[:, 22]], tbl_23[ids[:, 23]], tbl_24[ids[:, 24]], tbl_25[ids[:, 25]]], axis=1)
    z = _L0_rec_ref(r_dense_features, e)
    z = z.reshape(z.shape[0], -1)
    h = jnp.concatenate([z, r_dense_features], axis=1)
    h = jnp.maximum(h @ W_top1 + b_top1, 0.0)
    h = jnp.maximum(h @ W_top2 + b_top2, 0.0)
    y = h @ W_top3
    return y

_drawn_inputs = setup_inputs


def setup_inputs(seed=0):
    import zlib

    import numpy as np

    out = dict(_drawn_inputs(seed))
    spreads = {'b_top1': (0.0, 0.1), 'b_top2': (0.0, 0.1)}
    factors = {}
    for name, (base, spread) in spreads.items():
        noise = np.random.default_rng([zlib.crc32(name.encode()), seed]).standard_normal(out[name].shape)
        drawn = base * np.exp(spread * noise) if base else spread * noise
        out[name] = jnp.asarray(drawn.astype(out[name].dtype))
    for name, factor in factors.items():
        out[name] = (out[name] * factor).astype(out[name].dtype)
    return out
```

```python
import concourse.bass as bass
from concourse import mybir
from contextlib import ExitStack

P = 128
B, D = 512, 128
TABLES = 26
F = TABLES + 1
TILES = B // P
S, Q = 4, 32
ONEHOT = [2, 3, 4, 9, 10, 17, 18, 20]
NOH = len(ONEHOT)
OH_ROWS, OH_CHUNKS = 1000, 8
OH_K = OH_ROWS // OH_CHUNKS
GATHERED = [t for t in range(TABLES) if t not in ONEHOT]
NGA = len(GATHERED)
SLOTS = [t + 1 for t in ONEHOT] + [0] + [t + 1 for t in GATHERED]
DENSE_SLOT = NOH
GROUP = 4
GROUPS = [list(range(a, min(a + GROUP, F))) for a in range(DENSE_SLOT, F, GROUP)]
NG = len(GROUPS)
FP = 32
G1 = F - 1
PAIRS = F * (F - 1) // 2
PAIR_CHUNKS = 3
PC = PAIRS // PAIR_CHUNKS
H1, H2 = 512, 256
M1, M2 = H1 // P, H2 // P
QB = 4
GB = Q // QB
RAW_BUFS, PART_BUFS, OH_BUFS = 3, 2, 6


def pair_at(g):
    return g * (g - 1) // 2


def tower(nc, ids, ids_oh, dense, tables, w1_dense, w1_pairs, b1, w2, b2, w3, y):
    f32, f32r, i32 = mybir.dt.float32, mybir.dt.float32r, mybir.dt.int32
    ALU, ACT = mybir.AluOpType, mybir.ActivationFunctionType
    with ExitStack() as ctx:
        def sb(name, shape, dt=f32):
            return ctx.enter_context(nc.sbuf_tensor(name, shape, dt))

        def sem(name):
            return ctx.enter_context(nc.semaphore(name))

        ids_sb = sb("ids_sb", [P, TILES, TABLES], i32)
        ids_rep = sb("ids_rep", [P, NOH, B], i32)
        dense_sb = sb("dense_sb", [P, TILES, D])
        rows = sb("rows", [P, 2, NGA, D])
        feat = sb("feat", [P, TILES, Q, S, FP])
        ident = sb("ident", [P, P])
        row_no_i = sb("row_no_i", [P, OH_CHUNKS], i32)
        row_no = sb("row_no", [P, OH_CHUNKS])
        raw = sb("raw", [P, RAW_BUFS, OH_CHUNKS, D])
        hi = sb("hi", [P, PART_BUFS, OH_CHUNKS, D], f32r)
        lo = sb("lo", [P, PART_BUFS, OH_CHUNKS, D], f32r)
        onehot = sb("onehot", [P, OH_BUFS, B], f32r)
        gram = sb("gram", [P, Q, S, G1])
        pairs = sb("pairs", [Q, S, PAIRS])
        pairsT = sb("pairsT", [PC, PAIR_CHUNKS, P])
        wd = sb("wd", [P, 2, H1])
        wds = sb("wds", [P, H1])
        wp = sb("wp", [PC, PAIR_CHUNKS, H1])
        w2_sb = sb("w2_sb", [P, M1, H2])
        w3_sb = sb("w3_sb", [P, M2])
        b1_sb = sb("b1_sb", [P, M1])
        b2_sb = sb("b2_sb", [P, M2])
        h1 = sb("h1", [P, M1, P])
        h2 = sb("h2", [P, M2, P])
        y_sb = sb("y_sb", [1, B])

        ps = [ctx.enter_context(nc.psum_tensor(f"ps{i}", [P, 512], f32)) for i in range(8)]
        ps_feat = ps[0:2]
        ps_gram = ps[2:4]
        ps_pair = ps[4:6]
        ps_zt = ps[6]
        ps_mlp = ps[7]

        ids_landed, ids_oh_landed = sem("ids_landed"), [sem("ids_oh_landed0"), sem("ids_oh_landed1")]
        dense_landed, w1_landed, w23_landed = sem("dense_landed"), sem("w1_landed"), sem("w23_landed")
        raw_landed = [sem(f"raw_landed{i}") for i in range(RAW_BUFS)]
        rows_landed = [[sem(f"rows_landed{h}_{j}") for j in range(NG)] for h in range(2)]
        ident_ready, row_no_made, row_no_ready, pad_ready = (sem("ident_ready"), sem("row_no_made"),
                                                             sem("row_no_ready"), sem("pad_ready"))
        hi_ready, lo_ready, onehot_ready, onehot_used, lookup_out = (
            sem("hi_ready"), sem("lo_ready"), sem("onehot_ready"), sem("onehot_used"), sem("lookup_out"))
        feat_done, feat_out = sem("feat_done"), sem("feat_out")
        gram_done, gram_out_v, gram_out_a = sem("gram_done"), sem("gram_out_v"), sem("gram_out_a")
        pair_done, pair_out_v, pair_out_a = sem("pair_done"), sem("pair_out_v"), sem("pair_out_a")
        zt_done, zt_out, wds_ready = sem("zt_done"), sem("zt_out"), sem("wds_ready")
        h1a_done, h1b_done, h1a_out, h1b_out = sem("h1a_done"), sem("h1b_done"), sem("h1a_out"), sem("h1b_out")
        h2a_done, h2b_done, h2a_out, h2b_out = sem("h2a_done"), sem("h2b_done"), sem("h2a_out"), sem("h2b_out")
        y_done, y_out, y_stored = sem("y_done"), sem("y_out"), sem("y_stored")

        block = ctx.enter_context(nc.Block())

        @block.gpsimd
        def _(pool):
            pool.iota(row_no_i[:, :], pattern=[[1, OH_CHUNKS]], base=0,
                      channel_multiplier=OH_CHUNKS).then_inc(row_no_made, 1)
            pool.memset(ident[:, :], 0.0).then_inc(ident_ready, 1)
            pool.wait_ge(ident_ready, 1)
            pool.affine_select(out=ident[:, :], in_=ident[:, :], compare_op=ALU.not_equal, fill=1.0, base=0,
                               pattern=[[-1, P]], channel_multiplier=1).then_inc(ident_ready, 1)
            pool.wait_ge(ids_landed, 16)
            for t in range(TILES):
                for j, group in enumerate(GROUPS):
                    if t >= 2:
                        pool.wait_ge(feat_done, (t - 2) * NG + j + 1)
                    for slot in group:
                        if slot == DENSE_SLOT:
                            continue
                        table = SLOTS[slot] - 1
                        pool.indirect_dma_start(
                            out=rows[:, t % 2, slot - DENSE_SLOT - 1, :], out_offset=None, in_=tables[table],
                            in_offset=bass.IndirectOffsetOnAxis(ap=ids_sb[:, t, table:table + 1], axis=0),
                        ).then_inc(rows_landed[t % 2][j], 16)

        @block.sync
        def _(sp):
            sp.dma_start(ids_sb[:, :, :], ids.rearrange("(t p) f -> p t f", p=P)).then_inc(ids_landed, 16)
            sp.dma_start(ids_rep[:, 0, :], ids_oh[0, :].partition_broadcast(P)).then_inc(ids_oh_landed[0], 16)

            def load_table(i):
                src = tables[ONEHOT[i]].rearrange("(p c) d -> p c d", c=OH_CHUNKS)
                for a, b in ((0, 112), (112, OH_K)):
                    sp.dma_start(raw[a:b, i % RAW_BUFS], src[a:b]).then_inc(raw_landed[i % RAW_BUFS], 16)

            load_table(0)
            sp.dma_start(ids_rep[:, 1:NOH, :], ids_oh[1:NOH, :].partition_broadcast(P)).then_inc(ids_oh_landed[1], 16)
            load_table(1)
            sp.dma_start(dense_sb[:, :, :], dense.rearrange("(t p) d -> p t d", p=P)).then_inc(dense_landed, 16)
            load_table(2)
            for i in range(RAW_BUFS, NOH):
                sp.wait_ge(lo_ready, i - RAW_BUFS + 1)
                load_table(i)
            sp.dma_start(wd[:, :, :], w1_dense.rearrange("(k p) n -> p k n", p=P)).then_inc(w1_landed, 16)
            sp.dma_start(wp[:, :, :], w1_pairs.rearrange("(k p) n -> p k n", p=PC)).then_inc(w1_landed, 16)
            sp.dma_start(b1_sb[:, :], b1).then_inc(w1_landed, 16)
            sp.dma_start(w2_sb[:, :, :], w2.rearrange("(k p) n -> p k n", p=P)).then_inc(w23_landed, 16)
            sp.dma_start(w3_sb[:, :], w3).then_inc(w23_landed, 16)
            sp.dma_start(b2_sb[:, :], b2).then_inc(w23_landed, 16)
            sp.wait_ge(y_out, TILES)
            sp.dma_start(y.rearrange("b o -> o b"), y_sb[:, :]).then_inc(y_stored, 16)
            sp.wait_ge(y_stored, 16)

        @block.scalar
        def _(act):
            def high_part(i):
                act.wait_ge(raw_landed[i % RAW_BUFS], 32 * (i // RAW_BUFS + 1))
                if i >= PART_BUFS:
                    act.wait_ge(onehot_used, OH_CHUNKS * (i - PART_BUFS + 1))
                nc.scalar.activation(hi[0:OH_K, i % PART_BUFS], raw[0:OH_K, i % RAW_BUFS],
                                     ACT.Copy).then_inc(hi_ready, 1)

            def lookup_evacuate(i):
                act.wait_ge(onehot_used, OH_CHUNKS * (i + 1))
                nc.scalar.activation(
                    feat[:, :, :, :, i].rearrange("d t q s -> d t s q"),
                    ps_pair[i % 2][:, :].rearrange("d (t s q) -> d t s q", s=S, q=Q), ACT.Copy).then_inc(lookup_out, 1)

            def feat_evacuate(t, j):
                act.wait_ge(feat_done, t * NG + j + 1)
                a, k = GROUPS[j][0], len(GROUPS[j])
                nc.scalar.activation(
                    feat[:, t, :, :, a:a + k].rearrange("d q s f -> d f s q"),
                    ps_feat[(t * NG + j) % 2][:, 0:k * P].rearrange("d (f s q) -> d f s q", s=S, q=Q),
                    ACT.Copy).then_inc(feat_out, 1)

            def gram_evacuate(t, k):
                act.wait_ge(gram_done, t * GB + k + 1)
                nc.scalar.activation(gram[:, k * QB:(k + 1) * QB].rearrange("p q s g -> p (q s g)"),
                                     ps_gram[1][:, 0:QB * S * G1], ACT.Copy).then_inc(gram_out_a, 1)

            def pair_evacuate(t, s):
                act.wait_ge(pair_done, t * S + s + 1)
                nc.scalar.activation(pairs[:, s, :], ps_pair[1][0:Q, 0:PAIRS], ACT.Copy).then_inc(pair_out_a, 1)

            def h1_first_half(t):
                act.wait_ge(h1a_done, t + 1)
                if t == 0:
                    act.wait_ge(w1_landed, 48)
                for m in range(M1 // 2):
                    last = nc.scalar.activation(h1[:, m, :], ps_mlp[:, m * P:(m + 1) * P], ACT.Relu,
                                                bias=b1_sb[:, m:m + 1])
                last.then_inc(h1a_out, 1)

            def h2_first_half(t):
                act.wait_ge(h2a_done, t + 1)
                if t == 0:
                    act.wait_ge(w23_landed, 48)
                nc.scalar.activation(h2[:, 0, :], ps_mlp[:, 0:P], ACT.Relu, bias=b2_sb[:, 0:1]).then_inc(h2a_out, 1)

            high_part(0)
            high_part(1)
            for i in range(max(NOH, NG)):
                if i < NOH:
                    lookup_evacuate(i)
                    if i + 2 < NOH:
                        high_part(i + 2)
                if i < NG:
                    feat_evacuate(0, i)
            for t in range(TILES):
                more = t + 1 < TILES
                for k in range(1, GB // 2, 2):
                    gram_evacuate(t, k)
                if more:
                    feat_evacuate(t + 1, 0)
                for k in range(GB // 2 + 1, GB, 2):
                    gram_evacuate(t, k)
                if more:
                    feat_evacuate(t + 1, 1)
                if t:
                    h1_first_half(t - 1)
                for s in range(1, S, 2):
                    pair_evacuate(t, s)
                if more:
                    feat_evacuate(t + 1, 2)
                if t:
                    h2_first_half(t - 1)
                if more:
                    feat_evacuate(t + 1, 3)
                    feat_evacuate(t + 1, 4)
            h1_first_half(TILES - 1)
            h2_first_half(TILES - 1)

        @block.vector
        def _(dve):
            def low_part(i):
                dve.wait_ge(hi_ready, i + 1)
                if i >= PART_BUFS:
                    dve.wait_ge(onehot_used, OH_CHUNKS * (i - PART_BUFS + 1))
                nc.vector.tensor_tensor(lo[0:OH_K, i % PART_BUFS], raw[0:OH_K, i % RAW_BUFS],
                                        hi[0:OH_K, i % PART_BUFS].bitcast(f32), ALU.subtract).then_inc(lo_ready, 1)

            def one_hots(i):
                if i < 2:
                    dve.wait_ge(ids_oh_landed[i], 16)
                for c in range(OH_CHUNKS):
                    n = i * OH_CHUNKS + c
                    if n >= OH_BUFS:
                        dve.wait_ge(onehot_used, n - OH_BUFS + 1)
                    nc.vector.tensor_scalar(onehot[0:OH_K, n % OH_BUFS], ids_rep[0:OH_K, i],
                                            row_no[0:OH_K, c:c + 1], None, ALU.is_equal).then_inc(onehot_ready, 1)

            def gram_evacuate(t, k):
                dve.wait_ge(gram_done, t * GB + k + 1)
                nc.vector.tensor_copy(gram[:, k * QB:(k + 1) * QB].rearrange("p q s g -> p (q s g)"),
                                      ps_gram[0][:, 0:QB * S * G1]).then_inc(gram_out_v, 1)

            def pair_evacuate(t, s):
                dve.wait_ge(pair_done, t * S + s + 1)
                nc.vector.tensor_copy(pairs[:, s, :], ps_pair[0][0:Q, 0:PAIRS]).then_inc(pair_out_v, 1)

            def zt_evacuate(t):
                dve.wait_ge(zt_done, t + 1)
                nc.vector.tensor_copy(pairsT[:, :, :], ps_zt[0:PC, 0:PAIR_CHUNKS * P]
                                      .rearrange("p (c b) -> p c b", b=P)).then_inc(zt_out, 1)

            def h1_second_half(t):
                dve.wait_ge(h1b_done, t + 1)
                for m in range(M1 // 2, M1):
                    k = m - M1 // 2
                    last = nc.vector.tensor_scalar(h1[:, m, :], ps_zt[:, k * P:(k + 1) * P], b1_sb[:, m:m + 1], 0.0,
                                                   ALU.add, ALU.max)
                last.then_inc(h1b_out, 1)

            def h2_second_half(t):
                dve.wait_ge(h2b_done, t + 1)
                if t == 0:
                    dve.wait_ge(w23_landed, 48)
                nc.vector.tensor_scalar(h2[:, 1, :], ps_zt[:, 0:P], b2_sb[:, 1:2], 0.0,
                                        ALU.add, ALU.max).then_inc(h2b_out, 1)

            def y_evacuate(t):
                dve.wait_ge(y_done, t + 1)
                nc.vector.tensor_copy(y_sb[0:1, t * P:(t + 1) * P], ps_mlp[0:1, 0:P]).then_inc(y_out, 1)

            nc.vector.memset(feat[:, :, :, :, F:FP].rearrange("d t q s f -> d (t q s) f"), 0.0).then_inc(pad_ready, 1)
            dve.wait_ge(row_no_made, 1)
            nc.vector.tensor_copy(row_no[:, :], row_no_i[:, :]).then_inc(row_no_ready, 1)
            dve.wait_ge(row_no_ready, 1)
            for i in range(NOH):
                low_part(i)
                one_hots(i)
            dve.wait_ge(w1_landed, 48)
            nc.vector.tensor_tensor(wds[:, :], wd[:, 0, :], wd[:, 1, :], ALU.add).then_inc(wds_ready, 1)
            for t in range(TILES):
                for k in range(0, GB, 2):
                    gram_evacuate(t, k)
                if t:
                    h1_second_half(t - 1)
                for s in range(0, S, 2):
                    pair_evacuate(t, s)
                if t:
                    h2_second_half(t - 1)
                zt_evacuate(t)
                if t:
                    y_evacuate(t - 1)
            h1_second_half(TILES - 1)
            h2_second_half(TILES - 1)
            y_evacuate(TILES - 1)

        @block.tensor
        def _(pe):
            def lookup(i):
                if i >= 2:
                    pe.wait_ge(lookup_out, i - 1)
                pe.wait_ge(hi_ready, i + 1)
                pe.wait_ge(lo_ready, i + 1)
                for c in range(OH_CHUNKS):
                    n = i * OH_CHUNKS + c
                    pe.wait_ge(onehot_ready, n + 1)
                    nc.tensor.matmul(ps_pair[i % 2][:, :], hi[0:OH_K, i % PART_BUFS, c], onehot[0:OH_K, n % OH_BUFS],
                                     start=(c == 0), stop=False)
                    last = nc.tensor.matmul(ps_pair[i % 2][:, :], lo[0:OH_K, i % PART_BUFS, c],
                                            onehot[0:OH_K, n % OH_BUFS], start=False, stop=(c == OH_CHUNKS - 1))
                    last.then_inc(onehot_used, 1)

            def feat_transpose(t, j):
                n = t * NG + j
                if n >= 2:
                    pe.wait_ge(feat_out, n - 1)
                if j == 0 and t == 0:
                    pe.wait_ge(dense_landed, 16)
                pe.wait_ge(rows_landed[t % 2][j], 16 * (t // 2 + 1) * (len(GROUPS[j]) - (DENSE_SLOT in GROUPS[j])))
                for k, slot in enumerate(GROUPS[j]):
                    src = dense_sb[:, t, :] if slot == DENSE_SLOT else rows[:, t % 2, slot - DENSE_SLOT - 1, :]
                    last = nc.tensor.transpose(ps_feat[n % 2][:, k * P:(k + 1) * P], src, ident[:, :])
                last.then_inc(feat_done, 1)

            def gram_bank(t, k):
                n = t * GB + k
                if n >= 2:
                    pe.wait_ge((gram_out_v, gram_out_a)[n % 2], n // 2)
                for i in range(QB):
                    q = k * QB + i
                    last = nc.tensor.matmul(ps_gram[n % 2][:, i * S * G1:(i + 1) * S * G1],
                                            feat[:, t, q].rearrange("d s f -> d (s f)"), feat[:, t, q, :, 1:F],
                                            start=True, stop=True)
                last.then_inc(gram_done, 1)

            def pair_transpose(t, s):
                n = t * S + s
                if n >= 2:
                    pe.wait_ge((pair_out_v, pair_out_a)[n % 2], n // 2)
                for g in range(1, F):
                    last = nc.tensor.transpose(ps_pair[n % 2][0:Q, pair_at(g):pair_at(g) + g],
                                               gram[Q * s:Q * s + g, :, s, g - 1],
                                               ident[Q * s:Q * s + g, Q * s:Q * s + g])
                last.then_inc(pair_done, 1)

            def zt_transpose(t):
                pe.wait_ge(pair_out_v, 2 * (t + 1))
                pe.wait_ge(pair_out_a, 2 * (t + 1))
                if t:
                    pe.wait_ge(h2b_out, t)
                for s in range(S):
                    for c in range(PAIR_CHUNKS):
                        last = nc.tensor.transpose(ps_zt[0:PC, c * P + s * Q:c * P + (s + 1) * Q],
                                                   pairs[:, s, c * PC:(c + 1) * PC], ident[0:Q, 0:Q])
                last.then_inc(zt_done, 1)

            def layer1(t):
                if t == 0:
                    pe.wait_ge(wds_ready, 1)
                    pe.wait_ge(w1_landed, 48)
                pe.wait_ge(zt_out, t + 1)
                if t:
                    pe.wait_ge(y_out, t)
                dense_t = feat[:, t, :, :, DENSE_SLOT].rearrange("d q s -> d s q")
                for m in range(M1):
                    half, k = divmod(m, M1 // 2)
                    out = (ps_mlp, ps_zt)[half][:, k * P:(k + 1) * P]
                    nc.tensor.matmul(out, wds[:, m * P:(m + 1) * P], dense_t, start=True, stop=False)
                    for c in range(PAIR_CHUNKS):
                        last = nc.tensor.matmul(out, wp[:, c, m * P:(m + 1) * P], pairsT[:, c, :],
                                                start=False, stop=(c == PAIR_CHUNKS - 1))
                    if k == M1 // 2 - 1:
                        last.then_inc((h1a_done, h1b_done)[half], 1)

            def layer2(t):
                if t == 0:
                    pe.wait_ge(w23_landed, 48)
                pe.wait_ge(h1a_out, t + 1)
                pe.wait_ge(h1b_out, t + 1)
                for m in range(M2):
                    for c in range(M1):
                        last = nc.tensor.matmul((ps_mlp, ps_zt)[m][:, 0:P], w2_sb[:, c, m * P:(m + 1) * P], h1[:, c, :],
                                                start=(c == 0), stop=(c == M1 - 1))
                    last.then_inc((h2a_done, h2b_done)[m], 1)

            def layer3(t):
                pe.wait_ge(h2a_out, t + 1)
                pe.wait_ge(h2b_out, t + 1)
                for c in range(M2):
                    last = nc.tensor.matmul(ps_mlp[0:1, 0:P], w3_sb[:, c:c + 1], h2[:, c, :],
                                            start=(c == 0), stop=(c == M2 - 1))
                last.then_inc(y_done, 1)

            pe.wait_ge(ident_ready, 2)
            for i in range(max(NOH, NG)):
                if i < NOH:
                    lookup(i)
                if i < NG:
                    feat_transpose(0, i)
            pe.wait_ge(pad_ready, 1)
            pe.wait_ge(lookup_out, NOH)
            for t in range(TILES):
                more = t + 1 < TILES
                pe.wait_ge(feat_out, (t + 1) * NG)
                for k in range(GB // 2):
                    gram_bank(t, k)
                if more:
                    feat_transpose(t + 1, 0)
                for k in range(GB // 2, GB):
                    gram_bank(t, k)
                if more:
                    feat_transpose(t + 1, 1)
                if t:
                    layer1(t - 1)
                pe.wait_ge(gram_out_v, (t + 1) * GB // 2)
                pe.wait_ge(gram_out_a, (t + 1) * GB // 2)
                for s in range(S):
                    pair_transpose(t, s)
                if more:
                    feat_transpose(t + 1, 2)
                if t:
                    layer2(t - 1)
                zt_transpose(t)
                if more:
                    feat_transpose(t + 1, 3)
                if t:
                    layer3(t - 1)
                if more:
                    feat_transpose(t + 1, 4)
            layer1(TILES - 1)
            layer2(TILES - 1)
            layer3(TILES - 1)


def kernel(**inputs):
    import numpy as _np
    import concourse.bacc as _bacc
    from concourse import mybir as _mybir
    from concourse.bass_utils import run_bass_kernel_spmd as _run

    nc = _bacc.Bacc("TRN2", target_bir_lowering=False, num_devices=1)
    ids = _np.asarray(inputs["ids"])
    w1 = _np.asarray(inputs["W_top1"])
    reference_pair = {}
    for f in range(F):
        for g in range(f + 1, F):
            reference_pair[f, g] = len(reference_pair)
    order = [D + reference_pair[min(SLOTS[f], SLOTS[g]), max(SLOTS[f], SLOTS[g])] for g in range(1, F) for f in range(g)]
    laid = {
        "ids": ids,
        "ids_oh": ids[:, ONEHOT].T,
        "dense": inputs["r_dense_features"],
        **{f"tbl_{i}": inputs[f"tbl_{i}"] for i in range(TABLES)},
        "w1_dense": _np.concatenate([w1[0:D], w1[D + PAIRS:]], axis=0),
        "w1_pairs": w1[order],
        "b1": _np.asarray(inputs["b_top1"]).reshape(M1, P).T,
        "w2": inputs["W_top2"],
        "b2": _np.asarray(inputs["b_top2"]).reshape(M2, P).T,
        "w3": _np.asarray(inputs["W_top3"]).reshape(M2, P).T,
    }
    arrays, args = {}, {}
    for name, a in laid.items():
        a = _np.ascontiguousarray(a)
        arrays[f"in_{name}"] = a
        args[name] = nc.dram_tensor(f"in_{name}", a.shape, _mybir.dt.from_np(a.dtype), kind="ExternalInput").ap()
    args["tables"] = [args.pop(f"tbl_{i}") for i in range(TABLES)]
    out = nc.dram_tensor("y", (B, 1), _mybir.dt.float32, kind="ExternalOutput").ap()
    tower(nc, y=out, **args)
    r = _run(nc, [arrays], core_ids=[0])
    return r.results[0]["y"]
```

```python
import concourse.bass as bass
from concourse import mybir
from contextlib import ExitStack

P = 128
B, D = 512, 128
TABLES = 26
F = TABLES + 1
TILES = B // P
S, Q = 4, 32
BLOCK = 32
PER_DMA = P // BLOCK
BLOCKS = B // BLOCK
R = P // BLOCK
E = Q // R
ONEHOT = [2, 3, 4, 9, 10, 17]
NOH = len(ONEHOT)
OH_ROWS, OH_CHUNKS = 1000, 8
OH_K = OH_ROWS // OH_CHUNKS
GATHERED = [t for t in range(TABLES) if t not in ONEHOT]
NGA = len(GATHERED)
SLOTS = [t + 1 for t in ONEHOT] + [0] + [t + 1 for t in GATHERED]
DENSE_SLOT = NOH
DMAS = NGA // PER_DMA
GATHER_SLOT = DENSE_SLOT + 1
PARTS = [(0, DMAS - 1), (DMAS - 1, DMAS)]
ROW_BUFS = R
FP = 32
G1 = F - 1
PAIRS = F * (F - 1) // 2
PAIR_CHUNKS = 3
PC = PAIRS // PAIR_CHUNKS
H1, H2 = 512, 256
M1, M2 = H1 // P, H2 // P
QB = 4
BANKS = E // QB
RAW_BUFS, PART_BUFS = 3, 3
OH_BUFS, OH_BUFS_A = 10, 2
ACT_CHUNK = OH_CHUNKS - 1
HALF = OH_CHUNKS // 2


PACK = 5
STARTS = range(1, F - 1, PACK)


def rectangle(a):
    return [(f, g) for g in range(a, min(a + PACK, F)) for f in range(a)]


def diagonal(n):
    return [(a + i, a + i + n) for a in STARTS for i in range(PACK - n)]


PACKED = {}
ORDER = []
for part, members in ([(("rectangle", a), rectangle(a)) for a in (*STARTS, F - 1)]
                      + [(("diagonal", n), diagonal(n)) for n in range(1, PACK)]):
    PACKED[part] = len(ORDER)
    ORDER += members
assert len(ORDER) == len(set(ORDER)) == PAIRS
LATE = 14


def tower(nc, ids_gather, ids_oh, dense, tables, gather_tables, w1_dense, w1_pairs, b1, w2, b2, w3, y):
    f32, f32r, i32 = mybir.dt.float32, mybir.dt.float32r, mybir.dt.int32
    ALU, ACT = mybir.AluOpType, mybir.ActivationFunctionType
    with ExitStack() as ctx:
        def sb(name, shape, dt=f32):
            return ctx.enter_context(nc.sbuf_tensor(name, shape, dt))

        def sem(name):
            return ctx.enter_context(nc.semaphore(name))

        ids_sb = sb("ids_sb", [P, BLOCKS + 1, DMAS], i32)
        index = sb("index", [P, BLOCKS * DMAS], i32)
        ids_rep = sb("ids_rep", [P, NOH, B], i32)
        dense_sb = sb("dense_sb", [P, TILES, D])
        rows = sb("rows", [P, ROW_BUFS, DMAS, D])
        feat = sb("feat", [P, TILES, Q, S, FP])
        ident = sb("ident", [P, P])
        row_no_i = sb("row_no_i", [P, OH_CHUNKS], i32)
        row_no = sb("row_no", [P, OH_CHUNKS])
        minus_row_no = sb("minus_row_no", [P, 1])
        distance = sb("distance", [P, B])
        raw = sb("raw", [P, RAW_BUFS, OH_CHUNKS, D])
        hi = sb("hi", [P, PART_BUFS, OH_CHUNKS, D], f32r)
        lo = sb("lo", [P, PART_BUFS, OH_CHUNKS, D], f32r)
        onehot = sb("onehot", [P, OH_BUFS, B], f32r)
        onehot_a = sb("onehot_a", [P, OH_BUFS_A, B], f32r)
        gram = sb("gram", [P, 2, Q, G1])
        turned = sb("turned", [P, G1, Q])
        packed = sb("packed", [P, PAIRS])
        pairsT = sb("pairsT", [PC, PAIR_CHUNKS, P])
        wd = sb("wd", [P, 2, H1])
        wds = sb("wds", [P, H1])
        wp = sb("wp", [PC, PAIR_CHUNKS, H1])
        w2_sb = sb("w2_sb", [P, M1, H2])
        w3_sb = sb("w3_sb", [P, M2])
        b1_sb = sb("b1_sb", [P, M1])
        b2_sb = sb("b2_sb", [P, M2])
        h1 = sb("h1", [P, M1, P])
        h2 = sb("h2", [P, M2, P])
        y_sb = sb("y_sb", [1, B])

        BANK = 512
        ps = ctx.enter_context(nc.psum_tensor("ps", [P, 8, BANK], f32))
        ps_feat = [ps[:, 0], ps[:, 1]]
        ps_gram = [ps[:, 2:4], ps[:, 4:6]]
        ps_lookup = [ps[:, 4], ps[:, 5]]
        ps_zt = ps[:, 6]
        ps_mlp = ps[:, 7]

        ids_landed, ids_oh_landed = sem("ids_landed"), [sem(f"ids_oh_landed{i}") for i in range(NOH)]
        dense_landed, w1_landed, w23_landed = sem("dense_landed"), sem("w1_landed"), sem("w23_landed")
        raw_landed = [[sem(f"raw_landed{i}_{half}") for half in range(2)] for i in range(RAW_BUFS)]
        rows_landed = [[sem(f"rows_landed{h}_{j}") for j in range(len(PARTS))] for h in range(ROW_BUFS)]
        index_ready, dense_done, dense_out = sem("index_ready"), sem("dense_done"), sem("dense_out")
        distance_ready, onehot_ready_a = sem("distance_ready"), sem("onehot_ready_a")
        ident_ready, row_no_made, row_no_ready, pad_ready = (sem("ident_ready"), sem("row_no_made"),
                                                             sem("row_no_ready"), sem("pad_ready"))
        hi_ready, lo_ready, onehot_ready, onehot_used, lookup_out = (
            sem("hi_ready"), sem("lo_ready"), sem("onehot_ready"), sem("onehot_used"), sem("lookup_out"))
        feat_done, feat_out = sem("feat_done"), sem("feat_out")
        gram_done, gram_out_v, gram_out_a = sem("gram_done"), sem("gram_out_v"), sem("gram_out_a")
        turned_ready, packed_v, packed_a = sem("turned_ready"), sem("packed_v"), sem("packed_a")
        zt_done, zt_out, wds_ready = sem("zt_done"), sem("zt_out"), sem("wds_ready")
        h1a_done, h1b_done, h1a_out, h1b_out = sem("h1a_done"), sem("h1b_done"), sem("h1a_out"), sem("h1b_out")
        h2a_done, h2b_done, h2a_out, h2b_out = sem("h2a_done"), sem("h2b_done"), sem("h2a_out"), sem("h2b_out")
        y_done, y_out, y_stored = sem("y_done"), sem("y_out"), sem("y_stored")

        def pads(t0, t1):
            return feat[:, t0:t1, :, :, F:FP].rearrange("d t q s f -> d (t q s) f")

        def product_block(r, s, banks):
            products = ps_gram[r % 2][:, :, 0:QB * S * G1].rearrange("p k (i s g) -> p k i s g", s=S, g=G1)
            return products[s * Q:(s + 1) * Q, banks, :, s, :]

        def gram_block(t, r, s, banks):
            return gram[s * Q:(s + 1) * Q, t % 2, r * E:(r + 1) * E, :].rearrange(
                "p (k i) g -> p k i g", i=QB)[:, banks]

        def evacuations(t, r):
            if t * R + r == BLOCKS - 1:
                return [slice(k, k + 1) for k in range(BANKS)]
            return [slice(0, BANKS)]

        block = ctx.enter_context(nc.Block())

        @block.gpsimd
        def _(pool):
            pool.iota(row_no_i[:, :], pattern=[[1, OH_CHUNKS]], base=0,
                      channel_multiplier=OH_CHUNKS).then_inc(row_no_made, 1)
            pool.memset(ident[:, :], 0.0).then_inc(ident_ready, 1)
            pool.wait_ge(ident_ready, 1)
            pool.affine_select(out=ident[:, :], in_=ident[:, :], compare_op=ALU.not_equal, fill=1.0, base=0,
                               pattern=[[-1, P]], channel_multiplier=1).then_inc(ident_ready, 1)
            pool.memset(pads(0, TILES // 2), 0.0).then_inc(pad_ready, 1)
            pool.wait_ge(index_ready, 1)

            def gather_tile(t):
                for slot in range(R):
                    if t:
                        pool.wait_ge(feat_done, (t - 1) * R * len(PARTS) + (slot + 1) * len(PARTS))
                    for j, (a, b) in enumerate(PARTS):
                        for m in range(a, b):
                            pool.indirect_dma_start(
                                out=rows[:, slot, m, :], out_offset=None, in_=gather_tables,
                                in_offset=bass.IndirectOffsetOnAxis(
                                    ap=index[:, (t * R + slot) * DMAS + m:(t * R + slot) * DMAS + m + 1], axis=0),
                            ).then_inc(rows_landed[slot][j], 16)

            for t in range(TILES):
                gather_tile(t)

        @block.sync
        def _(sp):

            sp.dma_start(ids_sb[:, :, :], ids_gather).then_inc(ids_landed, 16)

            def load_ids(i):
                sp.dma_start(ids_rep[:, i, :], ids_oh[i, :].partition_broadcast(P)).then_inc(ids_oh_landed[i], 16)

            def load_table(i):
                src = tables[ONEHOT[i]].rearrange("(p c) d -> p c d", c=OH_CHUNKS)
                for half in range(2):
                    c = half * HALF
                    for a, b in ((0, 112), (112, OH_K)):
                        sp.dma_start(raw[a:b, i % RAW_BUFS, c:c + HALF],
                                     src[a:b, c:c + HALF]).then_inc(raw_landed[i % RAW_BUFS][half], 16)

            load_ids(0)
            load_table(0)
            load_ids(1)
            load_table(1)
            load_ids(2)
            sp.dma_start(dense_sb[:, :, :], dense.rearrange("(t p) d -> p t d", p=P)).then_inc(dense_landed, 16)
            load_table(2)
            for i in range(RAW_BUFS, NOH):
                load_ids(i)
            for i in range(RAW_BUFS, NOH):
                sp.wait_ge(lo_ready, 2 * (i - RAW_BUFS + 1))
                load_table(i)
            sp.dma_start(wd[:, :, :], w1_dense.rearrange("(k p) n -> p k n", p=P)).then_inc(w1_landed, 16)
            sp.dma_start(wp[:, :, :], w1_pairs.rearrange("(k p) n -> p k n", p=PC)).then_inc(w1_landed, 16)
            sp.dma_start(b1_sb[:, :], b1).then_inc(w1_landed, 16)
            sp.dma_start(w2_sb[:, :, :], w2.rearrange("(k p) n -> p k n", p=P)).then_inc(w23_landed, 16)
            sp.dma_start(w3_sb[:, :], w3).then_inc(w23_landed, 16)
            sp.dma_start(b2_sb[:, :], b2).then_inc(w23_landed, 16)
            sp.wait_ge(y_out, TILES)
            sp.dma_start(y.rearrange("b o -> o b"), y_sb[:, :]).then_inc(y_stored, 16)
            sp.wait_ge(y_stored, 16)

        @block.scalar
        def _(act):
            def high_part(i):
                if i >= PART_BUFS:
                    act.wait_ge(onehot_used, OH_CHUNKS * (i - PART_BUFS + 1))
                for half in range(2):
                    c = half * HALF
                    act.wait_ge(raw_landed[i % RAW_BUFS][half], 32 * (i // RAW_BUFS + 1))
                    nc.scalar.activation(hi[0:OH_K, i % PART_BUFS, c:c + HALF], raw[0:OH_K, i % RAW_BUFS, c:c + HALF],
                                         ACT.Copy).then_inc(hi_ready, 1)

            def lookup_evacuate(i):
                act.wait_ge(onehot_used, OH_CHUNKS * (i + 1))
                nc.scalar.activation(
                    feat[:, :, :, :, i].rearrange("d t (r e) s -> d (t r) s e", e=E),
                    ps_lookup[i % 2][:, :].rearrange("d (k s e) -> d k s e", s=S, e=E), ACT.Copy).then_inc(lookup_out, 1)

            def dense_evacuate():
                act.wait_ge(dense_done, 1)
                nc.scalar.activation(
                    feat[:, :, :, :, DENSE_SLOT].rearrange("d t (r e) s -> d (t r) s e", e=E),
                    ps_zt[:, :].rearrange("d (k s e) -> d k s e", s=S, e=E), ACT.Copy).then_inc(dense_out, 1)

            def one_hot(i):
                if i == 0:
                    act.wait_ge(row_no_ready, 2)
                act.wait_ge(ids_oh_landed[i], 16)
                if i >= OH_BUFS_A:
                    act.wait_ge(onehot_used, OH_CHUNKS * (i - OH_BUFS_A + 1))
                if i:
                    act.wait_ge(onehot_ready_a, i)
                nc.scalar.activation(distance[0:OH_K, :], ids_rep[0:OH_K, i], ACT.Abs,
                                     bias=minus_row_no[0:OH_K, :]).then_inc(distance_ready, 1)
                act.wait_ge(distance_ready, i + 1)
                nc.scalar.activation(onehot_a[0:OH_K, i % OH_BUFS_A], distance[0:OH_K, :], ACT.Relu, bias=1.0,
                                     scale=-1.0).then_inc(onehot_ready_a, 1)

            def feat_evacuate(k):
                t, r = divmod(k, R)
                for j, (a, b) in enumerate(PARTS):
                    act.wait_ge(feat_done, k * len(PARTS) + j + 1)
                    first = GATHER_SLOT + a * PER_DMA
                    nc.scalar.activation(
                        feat[:, t, r * E:(r + 1) * E, :, first:first + (b - a) * PER_DMA].rearrange("d e s f -> d f s e"),
                        ps_feat[j][:, 0:(b - a) * P].rearrange("d (f s e) -> d f s e", s=S, e=E),
                        ACT.Copy).then_inc(feat_out, 1)

            def gram_evacuate(t, r):
                if t >= 2:
                    act.wait_ge(turned_ready, 2 * (t - 1))
                for banks in evacuations(t, r):
                    act.wait_ge(gram_done, (t * R + r) * BANKS + banks.stop)
                    for s in range(S // 2):
                        last = nc.scalar.activation(gram_block(t, r, s, banks), product_block(r, s, banks), ACT.Copy)
                last.then_inc(gram_out_a, 1)

            def pack(t, starts, last):
                for a in starts:
                    n = min(PACK, F - a)
                    at = PACKED["rectangle", a]
                    step = nc.scalar.activation(packed[:, at:at + n * a].rearrange("p (g f) -> p g f", f=a),
                                                turned[:, a - 1:a - 1 + n, 0:a], ACT.Copy)
                if last:
                    step.then_inc(packed_a, 1)

            def pack_tile(t):
                act.wait_ge(turned_ready, 2 * t + 1)
                if t:
                    act.wait_ge(zt_done, t)
                pack(t, [a for a in (*STARTS, F - 1) if a >= LATE], False)
                act.wait_ge(turned_ready, 2 * t + 2)
                pack(t, [a for a in STARTS if a < LATE], True)

            def h1_first_half(t):
                act.wait_ge(h1a_done, t + 1)
                if t == 0:
                    act.wait_ge(w1_landed, 48)
                for m in range(M1 // 2):
                    last = nc.scalar.activation(h1[:, m, :], ps_mlp[:, m * P:(m + 1) * P], ACT.Relu,
                                                bias=b1_sb[:, m:m + 1])
                last.then_inc(h1a_out, 1)

            def h2_first_half(t):
                act.wait_ge(h2a_done, t + 1)
                if t == 0:
                    act.wait_ge(w23_landed, 48)
                nc.scalar.activation(h2[:, 0, :], ps_mlp[:, 0:P], ACT.Relu, bias=b2_sb[:, 0:1]).then_inc(h2a_out, 1)

            high_part(0)
            one_hot(0)
            high_part(1)
            for i in range(NOH):
                if i + 1 < NOH:
                    one_hot(i + 1)
                if i + 2 < NOH:
                    high_part(i + 2)
                lookup_evacuate(i)
                if i == 0:
                    dense_evacuate()
                else:
                    feat_evacuate(i - 1)
            for r in range(R):
                gram_evacuate(0, r)
            for t in range(1, TILES - 1):
                pack_tile(t - 1)
                gram_evacuate(t, 0)
                feat_evacuate(t * R + 1)
                gram_evacuate(t, 1)
                h1_first_half(t - 1)
                feat_evacuate(t * R + 2)
                h2_first_half(t - 1)
                feat_evacuate(t * R + 3)
                gram_evacuate(t, 2)
                gram_evacuate(t, 3)
                feat_evacuate((t + 1) * R)
            t = TILES - 1
            pack_tile(t - 1)
            gram_evacuate(t, 0)
            h1_first_half(t - 1)
            feat_evacuate(t * R + 1)
            h2_first_half(t - 1)
            gram_evacuate(t, 1)
            feat_evacuate(t * R + 2)
            gram_evacuate(t, 2)
            feat_evacuate(t * R + 3)
            gram_evacuate(t, 3)
            pack_tile(t)
            h1_first_half(t)
            h2_first_half(t)

        @block.vector
        def _(dve):
            def low_part(i, half):
                dve.wait_ge(hi_ready, 2 * i + half + 1)
                if i >= PART_BUFS:
                    dve.wait_ge(onehot_used, OH_CHUNKS * (i - PART_BUFS + 1))
                c = half * HALF
                nc.vector.tensor_tensor(lo[0:OH_K, i % PART_BUFS, c:c + HALF], raw[0:OH_K, i % RAW_BUFS, c:c + HALF],
                                        hi[0:OH_K, i % PART_BUFS, c:c + HALF].bitcast(f32),
                                        ALU.subtract).then_inc(lo_ready, 1)

            def one_hots(i, c0, c1):
                if c0 == 0:
                    dve.wait_ge(ids_oh_landed[i], 16)
                for c in range(c0, c1):
                    n = i * ACT_CHUNK + c
                    if n >= OH_BUFS:
                        old_i, old_c = divmod(n - OH_BUFS, ACT_CHUNK)
                        dve.wait_ge(onehot_used, old_i * OH_CHUNKS + old_c + 1)
                    nc.vector.tensor_scalar(onehot[0:OH_K, n % OH_BUFS], ids_rep[0:OH_K, i],
                                            row_no[0:OH_K, c:c + 1], None, ALU.is_equal).then_inc(onehot_ready, 1)

            def gram_evacuate(t, r):
                for banks in evacuations(t, r):
                    dve.wait_ge(gram_done, (t * R + r) * BANKS + banks.stop)
                    for s in range(S // 2, S):
                        last = nc.vector.tensor_copy(gram_block(t, r, s, banks), product_block(r, s, banks))
                last.then_inc(gram_out_v, 1)

            def turn(t):
                dve.wait_ge(gram_out_v, (t + 1) * R)
                dve.wait_ge(gram_out_a, (t + 1) * R)
                if t:
                    dve.wait_ge(packed_a, t)
                    dve.wait_ge(packed_v, t)
                for a, b in ((LATE, F), (1, LATE)):
                    nc.vector.transpose(turned[:, a - 1:b - 1, :], gram[:, t % 2, :, a - 1:b - 1]
                                        .rearrange("p q g -> p g q")).then_inc(turned_ready, 1)

            def pack_diagonals(t):
                dve.wait_ge(turned_ready, 2 * t + 2)
                if t:
                    dve.wait_ge(zt_done, t)
                for n in range(1, PACK):
                    at, k = PACKED["diagonal", n], PACK - n
                    last = nc.vector.tensor_copy(
                        packed[:, at:at + k * len(STARTS)].rearrange("p (k i) -> p k i", i=k),
                        bass.AP(tensor=turned, offset=n * Q + 1,
                                ap=[[G1 * Q, P], [PACK * (Q + 1), len(STARTS)], [Q + 1, k]]))
                last.then_inc(packed_v, 1)

            def zt_evacuate(t):
                dve.wait_ge(zt_done, t + 1)
                for a, b in ((0, 1), (1, PAIR_CHUNKS)):
                    nc.vector.tensor_copy(pairsT[:, a:b, :], ps_zt[0:PC, a * P:b * P]
                                          .rearrange("p (c b) -> p c b", b=P)).then_inc(zt_out, 1)

            def h1_second_half(t):
                dve.wait_ge(h1b_done, t + 1)
                for m in range(M1 // 2, M1):
                    k = m - M1 // 2
                    nc.vector.tensor_scalar(h1[:, m, :], ps_zt[:, k * P:(k + 1) * P], b1_sb[:, m:m + 1], 0.0,
                                            ALU.add, ALU.max).then_inc(h1b_out, 1)

            def h2_second_half(t):
                dve.wait_ge(h2b_done, t + 1)
                if t == 0:
                    dve.wait_ge(w23_landed, 48)
                nc.vector.tensor_scalar(h2[:, 1, :], ps_zt[:, 0:P], b2_sb[:, 1:2], 0.0,
                                        ALU.add, ALU.max).then_inc(h2b_out, 1)

            def y_evacuate(t):
                dve.wait_ge(y_done, t + 1)
                nc.vector.tensor_copy(y_sb[0:1, t * P:(t + 1) * P].rearrange("o (r s e) -> o s r e", r=R, s=S),
                                      ps_mlp[0:1, 0:P].rearrange("o (s r e) -> o s r e", s=S, r=R)).then_inc(y_out, 1)

            dve.wait_ge(row_no_made, 1)
            nc.vector.tensor_copy(row_no[:, :], row_no_i[:, :]).then_inc(row_no_ready, 1)
            dve.wait_ge(row_no_ready, 1)
            nc.vector.tensor_scalar(minus_row_no[:, :], row_no[:, ACT_CHUNK:ACT_CHUNK + 1], -1.0, None,
                                    ALU.mult).then_inc(row_no_ready, 1)
            nc.vector.memset(pads(TILES // 2, TILES), 0.0).then_inc(pad_ready, 1)
            dve.wait_ge(ids_landed, 16)
            nc.vector.tensor_tensor(index[:, :].rearrange("p (k m) -> p k m", m=DMAS), ids_sb[:, 0:BLOCKS, :],
                                    ids_sb[:, BLOCKS:BLOCKS + 1, :].to_broadcast([P, BLOCKS, DMAS]),
                                    ALU.add).then_inc(index_ready, 1)
            one_hots(0, 0, 3)
            low_part(0, 0)
            one_hots(0, 3, HALF)
            low_part(0, 1)
            one_hots(0, HALF, ACT_CHUNK)
            for i in range(1, NOH):
                one_hots(i, 0, 1)
                low_part(i, 0)
                one_hots(i, 1, HALF)
                low_part(i, 1)
                one_hots(i, HALF, ACT_CHUNK)
            dve.wait_ge(w1_landed, 48)
            nc.vector.tensor_tensor(wds[:, :], wd[:, 0, :], wd[:, 1, :], ALU.add).then_inc(wds_ready, 1)
            for r in range(R):
                gram_evacuate(0, r)
            for t in range(1, TILES - 1):
                turn(t - 1)
                pack_diagonals(t - 1)
                gram_evacuate(t, 0)
                zt_evacuate(t - 1)
                gram_evacuate(t, 1)
                h1_second_half(t - 1)
                h2_second_half(t - 1)
                gram_evacuate(t, 2)
                y_evacuate(t - 1)
                gram_evacuate(t, 3)
            t = TILES - 1
            turn(t - 1)
            pack_diagonals(t - 1)
            zt_evacuate(t - 1)
            gram_evacuate(t, 0)
            h1_second_half(t - 1)
            h2_second_half(t - 1)
            gram_evacuate(t, 1)
            y_evacuate(t - 1)
            gram_evacuate(t, 2)
            gram_evacuate(t, 3)
            turn(TILES - 1)
            pack_diagonals(TILES - 1)
            zt_evacuate(TILES - 1)
            h1_second_half(TILES - 1)
            h2_second_half(TILES - 1)
            y_evacuate(TILES - 1)

        @block.tensor
        def _(pe):
            def lookup(i):
                if i >= 2:
                    pe.wait_ge(lookup_out, i - 1)
                for c in range(OH_CHUNKS):
                    if c % HALF == 0:
                        pe.wait_ge(hi_ready, 2 * i + c // HALF + 1)
                        pe.wait_ge(lo_ready, 2 * i + c // HALF + 1)
                    if c == ACT_CHUNK:
                        pe.wait_ge(onehot_ready_a, i + 1)
                        matrix = onehot_a[0:OH_K, i % OH_BUFS_A]
                    else:
                        pe.wait_ge(onehot_ready, i * ACT_CHUNK + c + 1)
                        matrix = onehot[0:OH_K, (i * ACT_CHUNK + c) % OH_BUFS]
                    nc.tensor.matmul(ps_lookup[i % 2][:, :], hi[0:OH_K, i % PART_BUFS, c], matrix,
                                     start=(c == 0), stop=False)
                    last = nc.tensor.matmul(ps_lookup[i % 2][:, :], lo[0:OH_K, i % PART_BUFS, c], matrix,
                                            start=False, stop=(c == OH_CHUNKS - 1))
                    last.then_inc(onehot_used, 1)

            def dense_transpose():
                pe.wait_ge(dense_landed, 16)
                for t in range(TILES):
                    last = nc.tensor.transpose(ps_zt[:, t * P:(t + 1) * P], dense_sb[:, t, :], ident[:, :])
                last.then_inc(dense_done, 1)

            def feat_transpose(k):
                slot, use = k % ROW_BUFS, k // ROW_BUFS
                for j, (a, b) in enumerate(PARTS):
                    if k:
                        pe.wait_ge(feat_out, (k - 1) * len(PARTS) + j + 1)
                    pe.wait_ge(rows_landed[slot][j], 16 * (b - a) * (use + 1))
                    for m in range(a, b):
                        last = nc.tensor.transpose(ps_feat[j][:, (m - a) * P:(m - a + 1) * P], rows[:, slot, m, :],
                                                   ident[:, :])
                    last.then_inc(feat_done, 1)

            def gram_products(t, r):
                pe.wait_ge(feat_out, (t * R + r + 1) * len(PARTS))
                if t * R + r >= 2:
                    pe.wait_ge(gram_out_v, t * R + r - 1)
                    pe.wait_ge(gram_out_a, t * R + r - 1)
                for e in range(E):
                    q = r * E + e
                    bank, i = divmod(e, QB)
                    last = nc.tensor.matmul(ps_gram[r % 2][:, bank, i * S * G1:(i + 1) * S * G1],
                                            feat[:, t, q].rearrange("d s f -> d (s f)"), feat[:, t, q, :, 1:F],
                                            start=True, stop=True)
                    if i == QB - 1:
                        last.then_inc(gram_done, 1)

            def zt_transpose(t):
                pe.wait_ge(packed_v, t + 1)
                pe.wait_ge(packed_a, t + 1)
                if t:
                    pe.wait_ge(h2b_out, t)
                for c in range(PAIR_CHUNKS):
                    last = nc.tensor.transpose(ps_zt[0:PC, c * P:(c + 1) * P], packed[:, c * PC:(c + 1) * PC],
                                               ident[:, :])
                last.then_inc(zt_done, 1)

            def layer1(t):
                if t == 0:
                    pe.wait_ge(wds_ready, 1)
                    pe.wait_ge(w1_landed, 48)
                if t:
                    pe.wait_ge(y_out, t)
                dense_t = feat[:, t, :, :, DENSE_SLOT].rearrange("d q s -> d s q")
                for m in range(M1):
                    half, k = divmod(m, M1 // 2)
                    out = (ps_mlp, ps_zt)[half][:, k * P:(k + 1) * P]
                    nc.tensor.matmul(out, wds[:, m * P:(m + 1) * P], dense_t, start=True, stop=False)
                    for c in range(PAIR_CHUNKS):
                        if m == 0 and c < 2:
                            pe.wait_ge(zt_out, 2 * t + c + 1)
                        last = nc.tensor.matmul(out, wp[:, c, m * P:(m + 1) * P], pairsT[:, c, :],
                                                start=False, stop=(c == PAIR_CHUNKS - 1))
                    if k == M1 // 2 - 1:
                        last.then_inc((h1a_done, h1b_done)[half], 1)

            def layer2(t):
                if t == 0:
                    pe.wait_ge(w23_landed, 48)
                pe.wait_ge(h1a_out, t + 1)
                for m in range(M2):
                    for c in range(M1):
                        if m == 0 and c >= M1 // 2:
                            pe.wait_ge(h1b_out, t * M1 // 2 + c - M1 // 2 + 1)
                        last = nc.tensor.matmul((ps_mlp, ps_zt)[m][:, 0:P], w2_sb[:, c, m * P:(m + 1) * P], h1[:, c, :],
                                                start=(c == 0), stop=(c == M1 - 1))
                    last.then_inc((h2a_done, h2b_done)[m], 1)

            def layer3(t):
                pe.wait_ge(h2a_out, t + 1)
                pe.wait_ge(h2b_out, t + 1)
                for c in range(M2):
                    last = nc.tensor.matmul(ps_mlp[0:1, 0:P], w3_sb[:, c:c + 1], h2[:, c, :],
                                            start=(c == 0), stop=(c == M2 - 1))
                last.then_inc(y_done, 1)

            def stay_warm():
                pe.wait_ge(gram_out_v, BLOCKS - 1)
                pe.wait_ge(gram_out_a, BLOCKS - 1)
                for bank in range(2):
                    nc.tensor.matmul(ps_gram[(R - 2) % 2][:, bank], ident[:, :], wds[:, :], start=True, stop=True)

            pe.wait_ge(ident_ready, 2)
            for i in range(NOH):
                lookup(i)
                if i == 0:
                    dense_transpose()
                else:
                    feat_transpose(i - 1)
            pe.wait_ge(pad_ready, 2)
            pe.wait_ge(dense_out, 1)
            pe.wait_ge(lookup_out, NOH)

            for r in range(R):
                gram_products(0, r)
            for t in range(1, TILES - 1):
                gram_products(t, 0)
                feat_transpose(t * R + 1)
                zt_transpose(t - 1)
                gram_products(t, 1)
                layer1(t - 1)
                feat_transpose(t * R + 2)
                layer2(t - 1)
                feat_transpose(t * R + 3)
                gram_products(t, 2)
                layer3(t - 1)
                gram_products(t, 3)
                feat_transpose((t + 1) * R)
            t = TILES - 1
            zt_transpose(t - 1)
            gram_products(t, 0)
            layer1(t - 1)
            feat_transpose(t * R + 1)
            layer2(t - 1)
            gram_products(t, 1)
            feat_transpose(t * R + 2)
            layer3(t - 1)
            gram_products(t, 2)
            feat_transpose(t * R + 3)
            gram_products(t, 3)
            stay_warm()
            zt_transpose(t)
            layer1(t)
            layer2(t)
            layer3(t)


def kernel(**inputs):
    import numpy as _np
    import concourse.bacc as _bacc
    from concourse import mybir as _mybir
    from concourse.bass_utils import run_bass_kernel_spmd as _run

    nc = _bacc.Bacc("TRN2", target_bir_lowering=False, num_devices=1)
    ids = _np.asarray(inputs["ids"])
    w1 = _np.asarray(inputs["W_top1"])
    reference_pair = {}
    for f in range(F):
        for g in range(f + 1, F):
            reference_pair[f, g] = len(reference_pair)
    order = [D + reference_pair[min(SLOTS[f], SLOTS[g]), max(SLOTS[f], SLOTS[g])] for f, g in ORDER]
    gathered = ids[:, GATHERED]
    starts = _np.cumsum([0] + [inputs[f"tbl_{i}"].shape[0] for i in GATHERED[:-1]]).astype(_np.int32)
    laid = {
        "ids_gather": _np.concatenate([
            gathered.reshape(BLOCKS, BLOCK, DMAS, PER_DMA).transpose(3, 1, 0, 2).reshape(P, BLOCKS, DMAS),
            _np.repeat(starts.reshape(DMAS, PER_DMA).T, BLOCK, axis=0)[:, None, :]], axis=1),
        "gather_tables": _np.concatenate([_np.asarray(inputs[f"tbl_{i}"]) for i in GATHERED], axis=0),
        "ids_oh": ids[:, ONEHOT].T,
        "dense": inputs["r_dense_features"],
        **{f"tbl_{i}": inputs[f"tbl_{i}"] for i in ONEHOT},
        "w1_dense": _np.concatenate([w1[0:D], w1[D + PAIRS:]], axis=0),
        "w1_pairs": w1[order],
        "b1": _np.asarray(inputs["b_top1"]).reshape(M1, P).T,
        "w2": inputs["W_top2"],
        "b2": _np.asarray(inputs["b_top2"]).reshape(M2, P).T,
        "w3": _np.asarray(inputs["W_top3"]).reshape(M2, P).T,
    }
    arrays, args = {}, {}
    for name, a in laid.items():
        a = _np.ascontiguousarray(a)
        arrays[f"in_{name}"] = a
        args[name] = nc.dram_tensor(f"in_{name}", a.shape, _mybir.dt.from_np(a.dtype), kind="ExternalInput").ap()
    args["tables"] = {i: args.pop(f"tbl_{i}") for i in ONEHOT}
    out = nc.dram_tensor("y", (B, 1), _mybir.dt.float32, kind="ExternalOutput").ap()
    tower(nc, y=out, **args)
    r = _run(nc, [arrays], core_ids=[0])
    return r.results[0]["y"]
```

```python
import concourse.bass as bass
from concourse import mybir
from contextlib import ExitStack

P = 128
B, D = 512, 128
TABLES = 26
F = TABLES + 1
TILES = B // P
S, Q = 4, 32
BLOCK = 32
PER_DMA = P // BLOCK
BLOCKS = B // BLOCK
R = P // BLOCK
E = Q // R
ONEHOT = [2, 3, 4, 9, 10, 17, 18]
NOH = len(ONEHOT)
MIXED = 20
OH_ROWS, OH_CHUNKS = 1000, 8
OH_K = OH_ROWS // OH_CHUNKS
GATHERED = [t for t in range(TABLES) if t not in ONEHOT]
NGA = len(GATHERED)
NWIDE = NGA % PER_DMA
GATHERED.remove(MIXED)
GATHERED.insert(NWIDE - 1, MIXED)
LOOKUPS = ONEHOT + [MIXED]
MIXED_TILE = TILES // 2
SLOTS = [t + 1 for t in ONEHOT] + [0] + [t + 1 for t in GATHERED]
DENSE_SLOT = NOH
DMAS = NGA // PER_DMA
TILE_DMAS = NWIDE + R * DMAS
WIDE_SLOT = DENSE_SLOT + 1
GATHER_SLOT = WIDE_SLOT + NWIDE
PARTS = [(0, DMAS - 1), (DMAS - 1, DMAS)]
ROW_BUFS, WIDE_BUFS = R, 2
FP = 32
STATIONARY = (S - 1) * FP + F
G1 = F - 1
PAIRS = F * (F - 1) // 2
PAIR_CHUNKS = 3
PC = PAIRS // PAIR_CHUNKS
H1, H2 = 512, 256
M1, M2 = H1 // P, H2 // P
BANK = 512
QB = BANK // (S * G1)
BANKS = E // QB
WARM_UP = 9
RAW_BUFS, PART_BUFS = 3, 3
OH_BUFS, OH_BUFS_A = 10, 2
ACT_CHUNK = OH_CHUNKS - 1
HALF = OH_CHUNKS // 2


PACK = 5
STARTS = range(1, F - 1, PACK)


def rectangle(a):
    return [(f, g) for g in range(a, min(a + PACK, F)) for f in range(a)]


def diagonal(n):
    return [(a + i, a + i + n) for a in STARTS for i in range(PACK - n)]


PACKED = {}
ORDER = []
for part, members in ([(("rectangle", a), rectangle(a)) for a in (*STARTS, F - 1)]
                      + [(("diagonal", n), diagonal(n)) for n in range(1, PACK)]):
    PACKED[part] = len(ORDER)
    ORDER += members
assert len(ORDER) == len(set(ORDER)) == PAIRS
LATE = 14
assert (NOH, NWIDE, R, TILES) == (7, 3, 4, 4)


def wide_tables(t):
    return NWIDE if t < MIXED_TILE else NWIDE - 1


def lookup_rows(i):
    return slice(0 if i < NOH else MIXED_TILE * P, B)


def tower(nc, ids_gather, ids_oh, dense, tables, gather_tables, w1_dense, w1_pairs, b1, w2, b2, w3, y):
    f32, f32r, i32 = mybir.dt.float32, mybir.dt.float32r, mybir.dt.int32
    ALU, ACT = mybir.AluOpType, mybir.ActivationFunctionType
    with ExitStack() as ctx:
        def sb(name, shape, dt=f32):
            return ctx.enter_context(nc.sbuf_tensor(name, shape, dt))

        def sem(name):
            return ctx.enter_context(nc.semaphore(name))

        ids_sb = sb("ids_sb", [P, TILES + 1, TILE_DMAS], i32)
        index = sb("index", [P, TILES * TILE_DMAS], i32)
        ids_rep = sb("ids_rep", [P, NOH + 1, B], i32)
        dense_sb = sb("dense_sb", [P, TILES, D])
        wide = sb("wide", [P, WIDE_BUFS, NWIDE, D])
        rows = sb("rows", [P, ROW_BUFS, DMAS, D])
        feat = sb("feat", [P, TILES, Q, S, FP])
        ident = sb("ident", [P, P])
        row_no_i = sb("row_no_i", [P, OH_CHUNKS], i32)
        row_no = sb("row_no", [P, OH_CHUNKS])
        minus_row_no = sb("minus_row_no", [P, 1])
        distance = sb("distance", [P, B])
        raw = sb("raw", [P, RAW_BUFS, OH_CHUNKS, D])
        hi = sb("hi", [P, PART_BUFS, OH_CHUNKS, D], f32r)
        lo = sb("lo", [P, PART_BUFS, OH_CHUNKS, D], f32r)
        onehot = sb("onehot", [P, OH_BUFS, B], f32r)
        onehot_a = sb("onehot_a", [P, OH_BUFS_A, B], f32r)
        gram = sb("gram", [P, 2, Q, G1])
        turned = sb("turned", [P, G1, Q])
        packed = sb("packed", [P, PAIRS])
        pairsT = sb("pairsT", [PC, PAIR_CHUNKS, P])
        w1_dense_sb = sb("w1_dense_sb", [P, 2, H1])
        w1_dense_sum = sb("w1_dense_sum", [P, H1])
        w1_pairs_sb = sb("w1_pairs_sb", [PC, PAIR_CHUNKS, H1])
        w2_sb = sb("w2_sb", [P, M1, H2])
        w3_sb = sb("w3_sb", [P, M2])
        b1_sb = sb("b1_sb", [P, M1])
        b2_sb = sb("b2_sb", [P, M2])
        h1 = sb("h1", [P, M1, P])
        h2 = sb("h2", [P, M2, P])
        y_sb = sb("y_sb", [1, B])

        ps = ctx.enter_context(nc.psum_tensor("ps", [P, 8, BANK], f32))
        ps_feat = [ps[:, 0], ps[:, 1]]
        ps_gram = [ps[:, 2:4], ps[:, 4:6]]
        ps_zt = ps[:, 6]
        ps_mlp = ps[:, 7]
        ps_lookup = [ps[:, 4 + i % 2] for i in range(NOH)] + [ps_mlp]

        h1_sums = [[(ps_mlp, ps_zt)[m // (M1 // 2)][:, m % (M1 // 2) * P:(m % (M1 // 2) + 1) * P] for m in range(M1)]
                   for t in range(TILES - 1)]
        h1_sums.append([bank[:, 0:P] for bank in (*ps_feat, ps_gram[1][:, 0], ps_gram[1][:, 1])])
        ps_h2b = [ps_zt if t != TILES - 2 else ps_gram[0][:, 1] for t in range(TILES)]
        ps_y = [ps_mlp if t != TILES - 2 else ps_gram[0][:, 0] for t in range(TILES)]

        ids_landed, ids_oh_landed = sem("ids_landed"), [sem(f"ids_oh_landed{i}") for i in range(NOH + 1)]
        dense_landed, w1_landed, w23_landed = sem("dense_landed"), sem("w1_landed"), sem("w23_landed")
        raw_landed = [[sem(f"raw_landed{i}_{half}") for half in range(2)] for i in range(RAW_BUFS)]
        rows_landed = [[sem(f"rows_landed{i}_{j}") for j in range(len(PARTS))] for i in range(ROW_BUFS)]
        wide_landed = [sem(f"wide_landed{i}") for i in range(WIDE_BUFS)]
        ident_ready, pad_ready = sem("ident_ready"), sem("pad_ready")
        row_no_i_ready, row_no_ready, minus_row_no_ready = (sem("row_no_i_ready"), sem("row_no_ready"),
                                                            sem("minus_row_no_ready"))
        gram_pad_ready = sem("gram_pad_ready")
        index_ready, dense_weights_ready = sem("index_ready"), sem("dense_weights_ready")
        hi_ready, lo_ready, onehot_used = sem("hi_ready"), sem("lo_ready"), sem("onehot_used")
        onehot_ready, distance_ready, onehot_a_ready = sem("onehot_ready"), sem("distance_ready"), sem("onehot_a_ready")
        lookup_out, dense_done, dense_out = sem("lookup_out"), sem("dense_done"), sem("dense_out")
        wide_done, wide_out, feat_done, feat_out = sem("wide_done"), sem("wide_out"), sem("feat_done"), sem("feat_out")
        gram_done, gram_out_v, gram_out_a = sem("gram_done"), sem("gram_out_v"), sem("gram_out_a")
        turned_ready, packed_v, packed_a = sem("turned_ready"), sem("packed_v"), sem("packed_a")
        zt_done, zt_out = sem("zt_done"), sem("zt_out")
        h1a_done, h1b_done, h1a_out, h1b_out = sem("h1a_done"), sem("h1b_done"), sem("h1a_out"), sem("h1b_out")
        h2a_done, h2b_done, h2a_out, h2b_out = sem("h2a_done"), sem("h2b_done"), sem("h2a_out"), sem("h2b_out")
        y_done, y_out, y_stored = sem("y_done"), sem("y_out"), sem("y_stored")

        def slot_of_all_rows(slot):
            return feat[:, :, :, :, slot].rearrange("d t (r e) s -> d (t r) s e", e=E)

        def pads(t0, t1):
            return feat[:, t0:t1, :, :, F:FP].rearrange("d t q s f -> d (t q s) f")

        def band(s):
            return F if s == S - 1 else Q

        def product_block(r, s, banks):
            products = ps_gram[r % 2][:, :, 0:QB * S * G1].rearrange("p k (i s g) -> p k i s g", s=S, g=G1)
            return products[s * Q:s * Q + band(s), banks, :, s, :]

        def gram_block(t, r, s, banks):
            return gram[s * Q:s * Q + band(s), t % 2, r * E:(r + 1) * E, :].rearrange(
                "p (k i) g -> p k i g", i=QB)[:, banks]

        def evacuations(t, r):
            if t * R + r == BLOCKS - 1:
                return [slice(k, k + 1) for k in range(BANKS)]
            return [slice(0, BANKS)]

        block = ctx.enter_context(nc.Block())

        @block.gpsimd
        def _(pool):
            pool.iota(row_no_i[:, :], pattern=[[1, OH_CHUNKS]], base=0,
                      channel_multiplier=OH_CHUNKS).then_inc(row_no_i_ready, 1)
            pool.memset(ident[:, :], 0.0).then_inc(ident_ready, 1)
            pool.wait_ge(ident_ready, 1)
            pool.affine_select(out=ident[:, :], in_=ident[:, :], compare_op=ALU.not_equal, fill=1.0, base=0,
                               pattern=[[-1, P]], channel_multiplier=1).then_inc(ident_ready, 1)
            pool.memset(pads(0, TILES // 2), 0.0).then_inc(pad_ready, 1)
            pool.wait_ge(index_ready, 1)

            def gather(out, t, n):
                return pool.indirect_dma_start(
                    out=out, out_offset=None, in_=gather_tables,
                    in_offset=bass.IndirectOffsetOnAxis(ap=index[:, t * TILE_DMAS + n:t * TILE_DMAS + n + 1], axis=0))

            def gather_tile(t):
                if t >= WIDE_BUFS:
                    pool.wait_ge(wide_done, t - WIDE_BUFS + 1)
                for m in range(wide_tables(t)):
                    gather(wide[:, t % WIDE_BUFS, m, :], t, m).then_inc(wide_landed[t % WIDE_BUFS], 16)
                for slot in range(R):
                    if t:
                        pool.wait_ge(feat_done, (t - 1) * R * len(PARTS) + (slot + 1) * len(PARTS))
                    for j, (a, b) in enumerate(PARTS):
                        for m in range(a, b):
                            gather(rows[:, slot, m, :], t, NWIDE + slot * DMAS + m).then_inc(rows_landed[slot][j], 16)

            for t in range(TILES):
                gather_tile(t)

        @block.sync
        def _(sp):
            sp.dma_start(ids_sb[:, :, :], ids_gather).then_inc(ids_landed, 16)

            def load_ids(i):
                sp.dma_start(ids_rep[:, i, :], ids_oh[i, :].partition_broadcast(P)).then_inc(ids_oh_landed[i], 16)

            def load_table(i):
                src = tables[LOOKUPS[i]].rearrange("(p c) d -> p c d", c=OH_CHUNKS)
                for half in range(2):
                    c = half * HALF
                    for a, b in ((0, 112), (112, OH_K)):
                        sp.dma_start(raw[a:b, i % RAW_BUFS, c:c + HALF],
                                     src[a:b, c:c + HALF]).then_inc(raw_landed[i % RAW_BUFS][half], 16)

            load_ids(0)
            load_table(0)
            load_ids(1)
            load_table(1)
            load_ids(2)
            sp.dma_start(dense_sb[:, :, :], dense.rearrange("(t p) d -> p t d", p=P)).then_inc(dense_landed, 16)
            load_table(2)
            for i in range(RAW_BUFS, NOH + 1):
                load_ids(i)
                sp.wait_ge(lo_ready, 2 * (i - RAW_BUFS + 1))
                load_table(i)
            sp.dma_start(w1_dense_sb[:, :, :], w1_dense.rearrange("(k p) n -> p k n", p=P)).then_inc(w1_landed, 16)
            sp.dma_start(w1_pairs_sb[:, :, :], w1_pairs.rearrange("(k p) n -> p k n", p=PC)).then_inc(w1_landed, 16)
            sp.dma_start(b1_sb[:, :], b1).then_inc(w1_landed, 16)
            sp.dma_start(w2_sb[:, :, :], w2.rearrange("(k p) n -> p k n", p=P)).then_inc(w23_landed, 16)
            sp.dma_start(w3_sb[:, :], w3).then_inc(w23_landed, 16)
            sp.dma_start(b2_sb[:, :], b2).then_inc(w23_landed, 16)
            sp.wait_ge(y_out, TILES)
            sp.dma_start(y.rearrange("b o -> o b"), y_sb[:, :]).then_inc(y_stored, 16)
            sp.wait_ge(y_stored, 16)

        @block.scalar
        def _(act):
            def high_part(i):
                if i >= PART_BUFS:
                    act.wait_ge(onehot_used, OH_CHUNKS * (i - PART_BUFS + 1))
                for half in range(2):
                    c = half * HALF
                    act.wait_ge(raw_landed[i % RAW_BUFS][half], 32 * (i // RAW_BUFS + 1))
                    nc.scalar.activation(hi[0:OH_K, i % PART_BUFS, c:c + HALF], raw[0:OH_K, i % RAW_BUFS, c:c + HALF],
                                         ACT.Copy).then_inc(hi_ready, 1)

            def lookup_evacuate(i):
                act.wait_ge(onehot_used, OH_CHUNKS * (i + 1))
                slot, first = (i, 0) if i < NOH else (WIDE_SLOT + NWIDE - 1, MIXED_TILE * R)
                for a, b in ((0, R), (R, BLOCKS)) if i == NOH - 1 else ((first, BLOCKS),):
                    nc.scalar.activation(
                        slot_of_all_rows(slot)[:, a:b],
                        ps_lookup[i][:, (a - first) * BLOCK:(b - first) * BLOCK]
                        .rearrange("d (k s e) -> d k s e", s=S, e=E), ACT.Copy).then_inc(lookup_out, 1)

            def dense_evacuate():
                act.wait_ge(dense_done, 1)
                nc.scalar.activation(
                    slot_of_all_rows(DENSE_SLOT),
                    ps_zt[:, :].rearrange("d (k s e) -> d k s e", s=S, e=E), ACT.Copy).then_inc(dense_out, 1)

            def one_hot(i):
                if i == 0:
                    act.wait_ge(minus_row_no_ready, 1)
                act.wait_ge(ids_oh_landed[i], 16)
                if i >= OH_BUFS_A:
                    act.wait_ge(onehot_used, OH_CHUNKS * (i - OH_BUFS_A + 1))
                if i:
                    act.wait_ge(onehot_a_ready, i)
                batch = lookup_rows(i)
                nc.scalar.activation(distance[0:OH_K, batch], ids_rep[0:OH_K, i, batch], ACT.Abs,
                                     bias=minus_row_no[0:OH_K, :]).then_inc(distance_ready, 1)
                act.wait_ge(distance_ready, i + 1)
                nc.scalar.activation(onehot_a[0:OH_K, i % OH_BUFS_A, batch], distance[0:OH_K, batch], ACT.Relu,
                                     bias=1.0, scale=-1.0).then_inc(onehot_a_ready, 1)

            def wide_evacuate(t):
                act.wait_ge(wide_done, t + 1)
                for m in range(wide_tables(t)):
                    last = nc.scalar.activation(
                        slot_of_all_rows(WIDE_SLOT + m)[:, t * R:(t + 1) * R],
                        ps_feat[0][:, m * P:(m + 1) * P].rearrange("d (r s e) -> d r s e", s=S, e=E), ACT.Copy)
                last.then_inc(wide_out, 1)

            def feat_evacuate(k):
                t, r = divmod(k, R)
                for j, (a, b) in enumerate(PARTS):
                    act.wait_ge(feat_done, k * len(PARTS) + j + 1)
                    first = GATHER_SLOT + a * PER_DMA
                    nc.scalar.activation(
                        feat[:, t, r * E:(r + 1) * E, :, first:first + (b - a) * PER_DMA]
                        .rearrange("d e s f -> d f s e"),
                        ps_feat[j][:, 0:(b - a) * P].rearrange("d (f s e) -> d f s e", s=S, e=E),
                        ACT.Copy).then_inc(feat_out, 1)

            def gram_evacuate(t, r):
                if t >= 2:
                    act.wait_ge(turned_ready, 2 * (t - 1))
                for banks in evacuations(t, r):
                    act.wait_ge(gram_done, (t * R + r) * BANKS + banks.stop)
                    for s in range(S // 2):
                        last = nc.scalar.activation(gram_block(t, r, s, banks), product_block(r, s, banks), ACT.Copy)
                last.then_inc(gram_out_a, 1)

            def pack_rectangles(starts):
                for a in starts:
                    n = min(PACK, F - a)
                    at = PACKED["rectangle", a]
                    step = nc.scalar.activation(packed[:, at:at + n * a].rearrange("p (g f) -> p g f", f=a),
                                                turned[:, a - 1:a - 1 + n, 0:a], ACT.Copy)
                return step

            def pack_tile(t):
                act.wait_ge(turned_ready, 2 * t + 1)
                if t:
                    act.wait_ge(zt_done, t)
                pack_rectangles([a for a in (*STARTS, F - 1) if a >= LATE])
                act.wait_ge(turned_ready, 2 * t + 2)
                pack_rectangles([a for a in STARTS if a < LATE]).then_inc(packed_a, 1)

            def h1_first_half(t):
                act.wait_ge(h1a_done, t + 1)
                if t == 0:
                    act.wait_ge(w1_landed, 48)
                for m in range(M1 // 2):
                    last = nc.scalar.activation(h1[:, m, :], h1_sums[t][m], ACT.Relu,
                                                bias=b1_sb[:, m:m + 1])
                last.then_inc(h1a_out, 1)

            def h2_first_half(t):
                act.wait_ge(h2a_done, t + 1)
                if t == 0:
                    act.wait_ge(w23_landed, 48)
                nc.scalar.activation(h2[:, 0, :], ps_mlp[:, 0:P], ACT.Relu, bias=b2_sb[:, 0:1]).then_inc(h2a_out, 1)

            high_part(0)
            one_hot(0)
            high_part(1)
            for i in range(NOH):
                one_hot(i + 1)
                if i + 2 <= NOH:
                    high_part(i + 2)
                lookup_evacuate(i)
                if i == 0:
                    dense_evacuate()
                elif i == 2:
                    wide_evacuate(0)
                elif i > 2:
                    feat_evacuate(i - 3)
            gram_evacuate(0, 0)
            wide_evacuate(1)
            gram_evacuate(0, 1)
            feat_evacuate(R)
            lookup_evacuate(NOH)
            gram_evacuate(0, 2)
            feat_evacuate(R + 1)
            gram_evacuate(0, 3)
            pack_tile(0)
            gram_evacuate(1, 0)
            gram_evacuate(1, 1)
            feat_evacuate(R + 2)
            h1_first_half(0)
            feat_evacuate(R + 3)
            h2_first_half(0)
            wide_evacuate(2)
            gram_evacuate(1, 2)
            feat_evacuate(2 * R)
            gram_evacuate(1, 3)
            feat_evacuate(2 * R + 1)
            pack_tile(1)
            gram_evacuate(2, 0)
            gram_evacuate(2, 1)
            feat_evacuate(2 * R + 2)
            h1_first_half(1)
            feat_evacuate(2 * R + 3)
            h2_first_half(1)
            wide_evacuate(3)
            gram_evacuate(2, 2)
            feat_evacuate(3 * R)
            gram_evacuate(2, 3)
            pack_tile(2)
            feat_evacuate(3 * R + 1)
            gram_evacuate(3, 0)
            gram_evacuate(3, 1)
            h1_first_half(2)
            feat_evacuate(3 * R + 2)
            feat_evacuate(3 * R + 3)
            gram_evacuate(3, 2)
            gram_evacuate(3, 3)
            pack_tile(3)
            h2_first_half(2)
            h1_first_half(3)
            h2_first_half(3)

        @block.vector
        def _(dve):
            def low_part(i, half):
                dve.wait_ge(hi_ready, 2 * i + half + 1)
                if i >= PART_BUFS:
                    dve.wait_ge(onehot_used, OH_CHUNKS * (i - PART_BUFS + 1))
                c = half * HALF
                nc.vector.tensor_tensor(lo[0:OH_K, i % PART_BUFS, c:c + HALF], raw[0:OH_K, i % RAW_BUFS, c:c + HALF],
                                        hi[0:OH_K, i % PART_BUFS, c:c + HALF].bitcast(f32),
                                        ALU.subtract).then_inc(lo_ready, 1)

            def one_hots(i, c0, c1):
                if c0 == 0:
                    dve.wait_ge(ids_oh_landed[i], 16)
                for c in range(c0, c1):
                    n = i * ACT_CHUNK + c
                    if n >= OH_BUFS:
                        old_i, old_c = divmod(n - OH_BUFS, ACT_CHUNK)
                        dve.wait_ge(onehot_used, old_i * OH_CHUNKS + old_c + 1)
                    batch = lookup_rows(i)
                    nc.vector.tensor_scalar(onehot[0:OH_K, n % OH_BUFS, batch], ids_rep[0:OH_K, i, batch],
                                            row_no[0:OH_K, c:c + 1], None, ALU.is_equal).then_inc(onehot_ready, 1)

            def gram_evacuate(t, r):
                for banks in evacuations(t, r):
                    dve.wait_ge(gram_done, (t * R + r) * BANKS + banks.stop)
                    for s in range(S // 2, S):
                        last = nc.vector.tensor_copy(gram_block(t, r, s, banks), product_block(r, s, banks))
                last.then_inc(gram_out_v, 1)

            def turn(t):
                dve.wait_ge(gram_out_v, (t + 1) * R)
                dve.wait_ge(gram_out_a, (t + 1) * R)
                if t:
                    dve.wait_ge(packed_a, t)
                    dve.wait_ge(packed_v, t)
                for a, b in ((LATE, F), (1, LATE)):
                    nc.vector.transpose(turned[:, a - 1:b - 1, :], gram[:, t % 2, :, a - 1:b - 1]
                                        .rearrange("p q g -> p g q")).then_inc(turned_ready, 1)

            def pack_diagonals(t):
                dve.wait_ge(turned_ready, 2 * t + 2)
                if t:
                    dve.wait_ge(zt_done, t)
                for n in range(1, PACK):
                    at, k = PACKED["diagonal", n], PACK - n
                    last = nc.vector.tensor_copy(
                        packed[:, at:at + k * len(STARTS)].rearrange("p (k i) -> p k i", i=k),
                        bass.AP(tensor=turned, offset=n * Q + 1,
                                ap=[[G1 * Q, P], [PACK * (Q + 1), len(STARTS)], [Q + 1, k]]))
                last.then_inc(packed_v, 1)

            def zt_evacuate(t):
                dve.wait_ge(zt_done, t + 1)
                for a, b in ((0, 1), (1, PAIR_CHUNKS)):
                    nc.vector.tensor_copy(pairsT[:, a:b, :], ps_zt[0:PC, a * P:b * P]
                                          .rearrange("p (c b) -> p c b", b=P)).then_inc(zt_out, 1)

            def h1_second_half(t):
                for m in range(M1 // 2, M1):
                    dve.wait_ge(h1b_done, t + 1 + (m - M1 // 2 if t == TILES - 1 else 0))
                    nc.vector.tensor_scalar(h1[:, m, :], h1_sums[t][m], b1_sb[:, m:m + 1], 0.0,
                                            ALU.add, ALU.max).then_inc(h1b_out, 1)

            def h2_second_half(t):
                dve.wait_ge(h2b_done, t + 1)
                if t == 0:
                    dve.wait_ge(w23_landed, 48)
                nc.vector.tensor_scalar(h2[:, 1, :], ps_h2b[t][:, 0:P], b2_sb[:, 1:2], 0.0,
                                        ALU.add, ALU.max).then_inc(h2b_out, 1)

            def y_evacuate(t):
                dve.wait_ge(y_done, t + 1)
                nc.vector.tensor_copy(y_sb[0:1, t * P:(t + 1) * P].rearrange("o (r s e) -> o s r e", r=R, s=S),
                                      ps_y[t][0:1, 0:P].rearrange("o (s r e) -> o s r e", s=S, r=R)).then_inc(y_out, 1)

            dve.wait_ge(row_no_i_ready, 1)
            nc.vector.tensor_copy(row_no[:, :], row_no_i[:, :]).then_inc(row_no_ready, 1)
            dve.wait_ge(row_no_ready, 1)
            nc.vector.tensor_scalar(minus_row_no[:, :], row_no[:, ACT_CHUNK:ACT_CHUNK + 1], -1.0, None,
                                    ALU.mult).then_inc(minus_row_no_ready, 1)
            nc.vector.memset(pads(TILES // 2, TILES), 0.0).then_inc(pad_ready, 1)
            dve.wait_ge(ids_landed, 16)
            nc.vector.tensor_tensor(index[:, :].rearrange("p (t m) -> p t m", m=TILE_DMAS), ids_sb[:, 0:TILES, :],
                                    ids_sb[:, TILES:TILES + 1, :].to_broadcast([P, TILES, TILE_DMAS]),
                                    ALU.add).then_inc(index_ready, 1)
            one_hots(0, 0, 3)
            low_part(0, 0)
            one_hots(0, 3, HALF)
            low_part(0, 1)
            one_hots(0, HALF, ACT_CHUNK)
            for i in range(1, NOH):
                one_hots(i, 0, 1)
                low_part(i, 0)
                one_hots(i, 1, HALF)
                low_part(i, 1)
                one_hots(i, HALF, ACT_CHUNK)
            nc.vector.memset(gram[(S - 1) * Q:P], 0.0).then_inc(gram_pad_ready, 1)
            one_hots(NOH, 0, 1)
            low_part(NOH, 0)
            one_hots(NOH, 1, HALF)
            low_part(NOH, 1)
            dve.wait_ge(gram_pad_ready, 1)
            gram_evacuate(0, 0)
            one_hots(NOH, HALF, ACT_CHUNK)
            dve.wait_ge(w1_landed, 48)
            nc.vector.tensor_tensor(w1_dense_sum[:, :], w1_dense_sb[:, 0, :], w1_dense_sb[:, 1, :],
                                    ALU.add).then_inc(dense_weights_ready, 1)
            for r in range(1, R):
                gram_evacuate(0, r)
            for t in range(1, TILES - 1):
                turn(t - 1)
                pack_diagonals(t - 1)
                gram_evacuate(t, 0)
                gram_evacuate(t, 1)
                zt_evacuate(t - 1)
                h1_second_half(t - 1)
                h2_second_half(t - 1)
                gram_evacuate(t, 2)
                if t == 1:
                    y_evacuate(0)
                gram_evacuate(t, 3)
            turn(2)
            pack_diagonals(2)
            y_evacuate(1)
            gram_evacuate(3, 0)
            zt_evacuate(2)
            gram_evacuate(3, 1)
            h1_second_half(2)
            gram_evacuate(3, 2)
            gram_evacuate(3, 3)
            turn(3)
            pack_diagonals(3)
            h2_second_half(2)
            zt_evacuate(3)
            y_evacuate(2)
            h1_second_half(3)
            h2_second_half(3)
            y_evacuate(3)

        @block.tensor
        def _(pe):
            def lookup(i, chunks=range(OH_CHUNKS)):
                if 2 <= i < NOH:
                    pe.wait_ge(lookup_out, i - 1)
                batch = lookup_rows(i)
                out = ps_lookup[i][:, 0:batch.stop - batch.start]
                for c in chunks:
                    if c % HALF == 0:
                        pe.wait_ge(hi_ready, 2 * i + c // HALF + 1)
                    if c == ACT_CHUNK:
                        pe.wait_ge(onehot_a_ready, i + 1)
                        matrix = onehot_a[0:OH_K, i % OH_BUFS_A, batch]
                    else:
                        pe.wait_ge(onehot_ready, i * ACT_CHUNK + c + 1)
                        matrix = onehot[0:OH_K, (i * ACT_CHUNK + c) % OH_BUFS, batch]
                    nc.tensor.matmul(out, hi[0:OH_K, i % PART_BUFS, c], matrix,
                                     start=(c == 0), stop=False)
                    if c % HALF == 0:
                        pe.wait_ge(lo_ready, 2 * i + c // HALF + 1)
                    last = nc.tensor.matmul(out, lo[0:OH_K, i % PART_BUFS, c], matrix,
                                            start=False, stop=(c == OH_CHUNKS - 1))
                    last.then_inc(onehot_used, 1)

            def dense_transpose():
                pe.wait_ge(dense_landed, 16)
                for t in range(TILES):
                    last = nc.tensor.transpose(ps_zt[:, t * P:(t + 1) * P], dense_sb[:, t, :], ident[:, :])
                last.then_inc(dense_done, 1)

            def wide_transpose(t):
                if t:
                    pe.wait_ge(feat_out, (t * R - 1) * len(PARTS) + 1)
                landed = sum(wide_tables(u) for u in range(t % WIDE_BUFS, t + 1, WIDE_BUFS))
                pe.wait_ge(wide_landed[t % WIDE_BUFS], 16 * landed)
                for m in range(wide_tables(t)):
                    last = nc.tensor.transpose(ps_feat[0][:, m * P:(m + 1) * P], wide[:, t % WIDE_BUFS, m, :],
                                               ident[:, :])
                last.then_inc(wide_done, 1)

            def feat_transpose(k):
                slot, use = k % ROW_BUFS, k // ROW_BUFS
                for j, (a, b) in enumerate(PARTS):
                    if j == 0 and slot == 0:
                        pe.wait_ge(wide_out, use + 1)
                    elif k:
                        pe.wait_ge(feat_out, (k - 1) * len(PARTS) + j + 1)
                    pe.wait_ge(rows_landed[slot][j], 16 * (b - a) * (use + 1))
                    for m in range(a, b):
                        last = nc.tensor.transpose(ps_feat[j][:, (m - a) * P:(m - a + 1) * P], rows[:, slot, m, :],
                                                   ident[:, :])
                    last.then_inc(feat_done, 1)

            def gram_products(t, r, banks=range(BANKS)):
                pe.wait_ge(feat_out, (t * R + r + 1) * len(PARTS))
                if t * R + r >= 2:
                    pe.wait_ge(gram_out_v, t * R + r - 1)
                    pe.wait_ge(gram_out_a, t * R + r - 1)
                for e in range(E):
                    q = r * E + e
                    bank, i = divmod(e, QB)
                    if bank not in banks:
                        continue
                    last = nc.tensor.matmul(ps_gram[r % 2][0:STATIONARY, bank, i * S * G1:(i + 1) * S * G1],
                                            feat[:, t, q].rearrange("d s f -> d (s f)")[:, 0:STATIONARY],
                                            feat[:, t, q, :, 1:F],
                                            start=True, stop=True)
                    if i == QB - 1:
                        last.then_inc(gram_done, 1)

            def zt_transpose(t):
                pe.wait_ge(packed_v, t + 1)
                pe.wait_ge(packed_a, t + 1)
                if t == TILES - 1:
                    pe.wait_ge(h1b_out, t * M1 // 2)
                elif t:
                    pe.wait_ge(h2b_out, t)
                for c in range(PAIR_CHUNKS):
                    last = nc.tensor.transpose(ps_zt[0:PC, c * P:(c + 1) * P], packed[:, c * PC:(c + 1) * PC],
                                               ident[:, :])
                last.then_inc(zt_done, 1)

            def layer1_dense(t, m):
                dense_t = feat[:, t, :, :, DENSE_SLOT].rearrange("d q s -> d s q")
                nc.tensor.matmul(h1_sums[t][m], w1_dense_sum[:, m * P:(m + 1) * P], dense_t, start=True, stop=False)

            def layer1_pairs(t, m):
                for c in range(PAIR_CHUNKS):
                    if m == 0 and c < 2:
                        pe.wait_ge(zt_out, 2 * t + c + 1)
                    last = nc.tensor.matmul(h1_sums[t][m], w1_pairs_sb[:, c, m * P:(m + 1) * P], pairsT[:, c, :],
                                            start=False, stop=(c == PAIR_CHUNKS - 1))
                return last

            def layer1_first_half(t):
                if t == 0:
                    pe.wait_ge(lookup_out, NOH + 2)
                    pe.wait_ge(dense_weights_ready, 1)
                    pe.wait_ge(w1_landed, 48)
                else:
                    pe.wait_ge(y_out, t)
                for m in range(M1 // 2):
                    layer1_dense(t, m)
                    last = layer1_pairs(t, m)
                last.then_inc(h1a_done, 1)

            def layer1_second_half(t):
                for m in range(M1 // 2, M1):
                    layer1_dense(t, m)
                    last = layer1_pairs(t, m)
                last.then_inc(h1b_done, 1)

            def last_layer1_dense(units):
                pe.wait_ge(feat_out, BLOCKS * len(PARTS))
                pe.wait_ge(gram_out_v, BLOCKS)
                pe.wait_ge(gram_out_a, BLOCKS)
                for m in units:
                    layer1_dense(TILES - 1, m)

            def last_layer1_pairs():
                for m in range(M1):
                    last = layer1_pairs(TILES - 1, m)
                    if m >= M1 // 2:
                        last.then_inc(h1b_done, 1)
                    elif m == M1 // 2 - 1:
                        last.then_inc(h1a_done, 1)

            def layer2(t):
                if t == 0:
                    pe.wait_ge(w23_landed, 48)
                pe.wait_ge(h1a_out, t + 1)
                if t == TILES - 1:
                    pe.wait_ge(h2a_out, t)
                if t == TILES - 2:
                    pe.wait_ge(gram_out_v, BLOCKS - 1)
                    pe.wait_ge(gram_out_a, BLOCKS - 1)
                for m in range(M2):
                    for c in range(M1):
                        if m == 0 and c >= M1 // 2:
                            pe.wait_ge(h1b_out, t * M1 // 2 + c - M1 // 2 + 1)
                        last = nc.tensor.matmul((ps_mlp, ps_h2b[t])[m][:, 0:P], w2_sb[:, c, m * P:(m + 1) * P],
                                                h1[:, c, :], start=(c == 0), stop=(c == M1 - 1))
                    last.then_inc((h2a_done, h2b_done)[m], 1)

            def layer3(t):
                for c in range(M2):
                    pe.wait_ge((h2a_out, h2b_out)[c], t + 1)
                    last = nc.tensor.matmul(ps_y[t][0:1, 0:P], w3_sb[:, c:c + 1], h2[:, c, :],
                                            start=(c == 0), stop=(c == M2 - 1))
                last.then_inc(y_done, 1)

            def warm_up():
                for k in range(WARM_UP):
                    nc.tensor.matmul(ps_zt[:, 0:P], ident[:, :], ident[:, :], start=True, stop=True)

            pe.wait_ge(ident_ready, 2)
            warm_up()
            for i in range(NOH):
                lookup(i)
                if i == 0:
                    dense_transpose()
                elif i == 2:
                    wide_transpose(0)
                elif i > 2:
                    feat_transpose(i - 3)
            pe.wait_ge(pad_ready, 2)
            pe.wait_ge(dense_out, 1)
            pe.wait_ge(lookup_out, NOH)
            gram_products(0, 0)
            lookup(NOH, range(HALF))
            wide_transpose(1)
            pe.wait_ge(lookup_out, NOH + 1)
            gram_products(0, 1)
            feat_transpose(R)
            lookup(NOH, range(HALF, OH_CHUNKS))
            gram_products(0, 2)
            feat_transpose(R + 1)
            gram_products(0, 3)
            gram_products(1, 0)
            gram_products(1, 1)
            zt_transpose(0)
            feat_transpose(R + 2)
            layer1_first_half(0)
            layer1_second_half(0)
            feat_transpose(R + 3)
            layer2(0)
            wide_transpose(2)
            gram_products(1, 2)
            feat_transpose(2 * R)
            layer3(0)
            gram_products(1, 3)
            feat_transpose(2 * R + 1)
            gram_products(2, 0)
            gram_products(2, 1)
            zt_transpose(1)
            feat_transpose(2 * R + 2)
            layer1_first_half(1)
            layer1_second_half(1)
            feat_transpose(2 * R + 3)
            layer2(1)
            wide_transpose(3)
            gram_products(2, 2)
            feat_transpose(3 * R)
            gram_products(2, 3)
            layer3(1)
            gram_products(3, 0)
            feat_transpose(3 * R + 1)
            zt_transpose(2)
            gram_products(3, 1)
            layer1_first_half(2)
            feat_transpose(3 * R + 2)
            layer1_second_half(2)
            gram_products(3, 2, banks=[0])
            feat_transpose(3 * R + 3)
            gram_products(3, 2, banks=[1])
            gram_products(3, 3)
            layer2(2)
            last_layer1_dense(range(M1 - 1))
            zt_transpose(3)
            layer3(2)
            last_layer1_dense([M1 - 1])
            last_layer1_pairs()
            layer2(3)
            layer3(3)


def kernel(**inputs):
    import numpy as _np
    import concourse.bacc as _bacc
    from concourse import mybir as _mybir
    from concourse.bass_utils import run_bass_kernel_spmd as _run

    nc = _bacc.Bacc("TRN2", target_bir_lowering=False, num_devices=1)
    ids = _np.asarray(inputs["ids"])
    w1 = _np.asarray(inputs["W_top1"])
    reference_pair = {}
    for f in range(F):
        for g in range(f + 1, F):
            reference_pair[f, g] = len(reference_pair)
    order = [D + reference_pair[min(SLOTS[f], SLOTS[g]), max(SLOTS[f], SLOTS[g])] for f, g in ORDER]
    by_tile = ids[:, GATHERED].reshape(TILES, P, NGA)
    wide = by_tile[:, :, :NWIDE].transpose(1, 0, 2)
    blocks = (by_tile[:, :, NWIDE:].reshape(TILES, R, BLOCK, DMAS, PER_DMA).transpose(4, 2, 0, 1, 3)
              .reshape(P, TILES, R * DMAS))
    starts = _np.cumsum([0] + [inputs[f"tbl_{i}"].shape[0] for i in GATHERED[:-1]]).astype(_np.int32)
    starts_wide = _np.tile(starts[:NWIDE], (P, 1))
    starts_blocks = _np.tile(_np.repeat(starts[NWIDE:].reshape(DMAS, PER_DMA).T, BLOCK, axis=0), (1, R))
    laid = {
        "ids_gather": _np.concatenate([
            _np.concatenate([wide, blocks], axis=2),
            _np.concatenate([starts_wide, starts_blocks], axis=1)[:, None, :]], axis=1),
        "gather_tables": _np.concatenate([_np.asarray(inputs[f"tbl_{i}"]) for i in GATHERED], axis=0),
        "ids_oh": ids[:, LOOKUPS].T,
        "dense": inputs["r_dense_features"],
        **{f"tbl_{i}": inputs[f"tbl_{i}"] for i in LOOKUPS},
        "w1_dense": _np.concatenate([w1[0:D], w1[D + PAIRS:]], axis=0),
        "w1_pairs": w1[order],
        "b1": _np.asarray(inputs["b_top1"]).reshape(M1, P).T,
        "w2": inputs["W_top2"],
        "b2": _np.asarray(inputs["b_top2"]).reshape(M2, P).T,
        "w3": _np.asarray(inputs["W_top3"]).reshape(M2, P).T,
    }
    arrays, args = {}, {}
    for name, a in laid.items():
        a = _np.ascontiguousarray(a)
        arrays[f"in_{name}"] = a
        args[name] = nc.dram_tensor(f"in_{name}", a.shape, _mybir.dt.from_np(a.dtype), kind="ExternalInput").ap()
    args["tables"] = {i: args.pop(f"tbl_{i}") for i in LOOKUPS}
    out = nc.dram_tensor("y", (B, 1), _mybir.dt.float32, kind="ExternalOutput").ap()
    tower(nc, y=out, **args)
    r = _run(nc, [arrays], core_ids=[0])
    return r.results[0]["y"]
```
